# Optimizing a Trainium2 kernel written in Bass

```python
import numpy as np
import jax
import jax.numpy as jnp

def _softmax(x, axis=-1):
    return jax.nn.softmax(x, axis=axis)

def _gelu(x):
    return jax.nn.gelu(x, approximate=True)

def _silu(x):
    return jax.nn.silu(x)

def _sigmoid(x):
    return jax.nn.sigmoid(x)

def _layernorm(x, axis=-1, eps=1e-05):
    m = jnp.mean(x, axis=axis, keepdims=True)
    v = jnp.var(x, axis=axis, keepdims=True)
    return (x - m) / jnp.sqrt(v + eps)

def _scatter_add(tgt, idx, src, axis=0):
    return tgt.at[idx].add(src)

def _segment_sum(src, seg, n):
    return jax.ops.segment_sum(src, seg, n)
kernel_name = 'mk_macaron_d1_jaxref_r8_386d3d'

def setup_inputs(seed: int=0):
    np.random.seed(seed)
    _w = jnp.asarray

    def _L0_attn_setup():
        import jax, jax.numpy as jnp
        import numpy as np
        HEADS = 16
        DIM_HEADS = 64
        NUM_BUCKETS = 32
        MAX_DISTANCE = 128

        def _relative_position_bucket(rel_pos, num_buckets=NUM_BUCKETS, max_distance=MAX_DISTANCE):
            n = jnp.maximum(-rel_pos, 0)
            max_exact = num_buckets // 2
            is_small = n < max_exact
            nf = jnp.maximum(n, 1).astype(jnp.float32)
            val_if_large = max_exact + (jnp.log(nf / max_exact) / np.log(max_distance / max_exact) * (num_buckets - max_exact)).astype(jnp.int32)
            val_if_large = jnp.minimum(val_if_large, num_buckets - 1)
            return jnp.where(is_small, n, val_if_large)
        key = jax.random.key(seed)
        ks = jax.random.split(key, 6)
        B, N, D = (2, 256, 128)
        inner = HEADS * DIM_HEADS
        x = jax.random.normal(ks[0], (B, N, D), dtype=jnp.float32)
        Wq = jax.random.normal(ks[1], (D, inner), dtype=jnp.float32) * 0.02
        Wkv = jax.random.normal(ks[2], (D, 2 * DIM_HEADS), dtype=jnp.float32) * 0.02
        Wout = jax.random.normal(ks[3], (inner, D), dtype=jnp.float32) * 0.02
        bout = jnp.zeros((D,), dtype=jnp.float32)
        rel_emb = jax.random.normal(ks[4], (NUM_BUCKETS, HEADS), dtype=jnp.float32) * 0.02
        return {'x': x, 'Wq': Wq, 'Wkv': Wkv, 'Wout': Wout, 'bout': bout, 'rel_emb': rel_emb}
    _L0_attn_in = _L0_attn_setup()

    def _L0_ffn_setup():
        import jax, jax.numpy as jnp
        import numpy as np
        E = 8
        K = 2
        D = 128
        key = jax.random.key(seed)
        k0, k1, k2, k3 = jax.random.split(key, 4)
        x = jax.random.normal(k0, (2, 256, D), dtype=jnp.float32)
        gate_w = jax.random.normal(k1, (D, E), dtype=jnp.float32) * 0.02
        fc_w = jax.random.normal(k2, (E, D, 4 * D), dtype=jnp.float32) * 0.02
        proj_w = jax.random.normal(k3, (E, 4 * D, D), dtype=jnp.float32) * 0.02
        return {'x': x, 'gate_w': gate_w, 'fc_w': fc_w, 'proj_w': proj_w}
    _L0_ffn_in = _L0_ffn_setup()
    _d = {'L0_attn_x': _L0_attn_in['x'], 'L0_attn_Wq': _L0_attn_in['Wq'], 'L0_attn_Wkv': _L0_attn_in['Wkv'], 'L0_attn_Wout': _L0_attn_in['Wout'], 'L0_attn_bout': _L0_attn_in['bout'], 'L0_attn_rel_emb': _L0_attn_in['rel_emb'], 'L0_ffn_gate_w': _L0_ffn_in['gate_w'], 'L0_ffn_fc_w': _L0_ffn_in['fc_w'], 'L0_ffn_proj_w': _L0_ffn_in['proj_w']}
    _x0 = _d['L0_attn_x']
    _d['L0_attn_x'] = jax.random.normal(jax.random.fold_in(jax.random.key(seed), 1), (8, 512, 128), dtype=_x0.dtype)
    del _x0
    return _d

def reference(L0_attn_x, L0_attn_Wq, L0_attn_Wkv, L0_attn_Wout, L0_attn_bout, L0_attn_rel_emb, L0_ffn_gate_w, L0_ffn_fc_w, L0_ffn_proj_w):

    def _L0_attn_ref(x, Wq, Wkv, Wout, bout, rel_emb):
        import jax, jax.numpy as jnp
        import numpy as np
        HEADS = 16
        DIM_HEADS = 64
        NUM_BUCKETS = 32
        MAX_DISTANCE = 128

        def _relative_position_bucket(rel_pos, num_buckets=NUM_BUCKETS, max_distance=MAX_DISTANCE):
            n = jnp.maximum(-rel_pos, 0)
            max_exact = num_buckets // 2
            is_small = n < max_exact
            nf = jnp.maximum(n, 1).astype(jnp.float32)
            val_if_large = max_exact + (jnp.log(nf / max_exact) / np.log(max_distance / max_exact) * (num_buckets - max_exact)).astype(jnp.int32)
            val_if_large = jnp.minimum(val_if_large, num_buckets - 1)
            return jnp.where(is_small, n, val_if_large)
        B, N, D = x.shape
        h, dh = (HEADS, DIM_HEADS)
        scale = dh ** (-0.5)
        bias_scale = dh ** 0.5
        q = (x @ Wq).reshape(B, N, h, dh).transpose(0, 2, 1, 3) * scale
        kv = x @ Wkv
        k, v = (kv[..., :dh], kv[..., dh:])
        sim = jnp.einsum('bhid,bjd->bhij', q, k)
        pos = jnp.arange(N, dtype=jnp.int32)
        rel_pos = pos[None, :] - pos[:, None]
        rp_bucket = _relative_position_bucket(rel_pos)
        bias = rel_emb[rp_bucket]
        sim = sim + bias.transpose(2, 0, 1)[None] * bias_scale
        causal = jnp.triu(jnp.ones((N, N), dtype=bool), k=1)
        sim = jnp.where(causal[None, None], -jnp.finfo(sim.dtype).max, sim)
        attn = jax.nn.softmax(sim, axis=-1)
        out = jnp.einsum('bhij,bjd->bhid', attn, v)
        out = out.transpose(0, 2, 1, 3).reshape(B, N, h * dh)
        return out @ Wout + bout

    def _L0_ffn_ref(x, gate_w, fc_w, proj_w):
        import jax, jax.numpy as jnp
        import numpy as np
        E = 8
        K = 2
        D = 128
        orig_shape = x.shape
        d = orig_shape[-1]
        xt = x.reshape(-1, d)
        gates = jax.nn.softmax(xt @ gate_w, axis=-1)
        top_v, top_i = jax.lax.top_k(gates, K)
        top_v = top_v / jnp.sum(top_v, axis=-1, keepdims=True)
        h = jnp.einsum('nd,edf->enf', xt, fc_w)
        h = jax.nn.gelu(h, approximate=False)
        eo = jnp.einsum('enf,efd->end', h, proj_w)
        eo_nt = jnp.swapaxes(eo, 0, 1)
        sel = jnp.take_along_axis(eo_nt, top_i[:, :, None], axis=1)
        out = jnp.sum(sel * top_v[:, :, None], axis=1)
        return out.reshape(orig_shape)
    x = L0_attn_x
    x = x + 0.5 * _L0_ffn_ref(_layernorm(x, axis=-1), L0_ffn_gate_w, L0_ffn_fc_w, L0_ffn_proj_w)
    x = x + _L0_attn_ref(_layernorm(x, axis=-1), L0_attn_Wq, L0_attn_Wkv, L0_attn_Wout, L0_attn_bout, L0_attn_rel_emb)
    x = x + 0.5 * _L0_ffn_ref(_layernorm(x, axis=-1), L0_ffn_gate_w, L0_ffn_fc_w, L0_ffn_proj_w)
    return x

_drawn_inputs = setup_inputs


def setup_inputs(seed=0):
    import zlib

    import numpy as np

    out = dict(_drawn_inputs(seed))
    spreads = {'L0_attn_bout': (0.0, 0.1)}
    factors = {'L0_attn_Wq': 8.0, 'L0_attn_Wkv': 3.43, 'L0_attn_Wout': 3.478, 'L0_attn_rel_emb': 8.0}
    for name, (base, spread) in spreads.items():
        noise = np.random.default_rng([zlib.crc32(name.encode()), seed]).standard_normal(out[name].shape)
        drawn = base * np.exp(spread * noise) if base else spread * noise
        out[name] = jnp.asarray(drawn.astype(out[name].dtype))
    for name, factor in factors.items():
        out[name] = (out[name] * factor).astype(out[name].dtype)
    return out
```

```python
from contextlib import ExitStack

import math

import numpy as np

import concourse.bass as bass
from concourse import mybir

P = 128
D = 128
BATCH, SEQ = 8, 512
TILES = BATCH * SEQ // P
E, TOPK, F = 8, 2, 512
FC = F // P
ETILES = TILES * TOPK + E
PAIRS = TILES * TOPK
H, DH = 16, 64
HG, NG = 4, 4
QT = SEQ // P
BUCKETS, MAX_DISTANCE = 32, 128
EPS = 1e-5
MASKED = -3.0e38

F32 = mybir.dt.float32
F32R = mybir.dt.float32r
BF16 = mybir.dt.bfloat16
I32 = mybir.dt.int32
ALU = mybir.AluOpType
ACT = mybir.ActivationFunctionType
AX = mybir.AxisListType.X
ds = bass.ds


def bucket(n):
    exact = BUCKETS // 2
    if n < exact:
        return n
    large = exact + int(math.log(n / exact) / math.log(MAX_DISTANCE / exact) * (BUCKETS - exact))
    return min(large, BUCKETS - 1)


def bucket_runs():
    runs = []
    for n in range(SEQ):
        if runs and runs[-1][0] == bucket(n):
            runs[-1][2] = n + 1
        else:
            runs.append([bucket(n), n, n + 1])
    return runs


def build(nc, x, Wq, Wkv, Wout, bout, rel_emb, gate_w, fc_w, proj_w, out, stop=99):
    ctx = ExitStack()
    with ctx:
        def sb(name, shape, dt=F32):
            return ctx.enter_context(nc.sbuf_tensor(name, shape, dt))

        def sem(name):
            return ctx.enter_context(nc.semaphore(name))

        xn_dram = [nc.dram_tensor(f"xn_dram{r}", [TILES * P, D], F32).ap() for r in range(2)]
        y2_dram = [nc.dram_tensor(f"y2_dram{r}", [TILES * P * TOPK, D], F32).ap() for r in range(2)]
        ROW = SEQ + P
        bias_dram = nc.dram_tensor("bias_dram", [H, P, ROW], F32).ap()

        x_sb = sb("x_sb", [P, TILES, D])
        ident = sb("ident", [P, P])
        ones_bf = sb("ones_bf", [P, P], BF16)
        before = sb("before", [P, P], BF16)
        iota_p = sb("iota_p", [P, P])
        pair_val = sb("pair_val", [P, TOPK])
        tile_val = sb("tile_val", [P, PAIRS])
        rev8 = sb("rev8", [P, E])
        tile_start = sb("tile_start", [P, ETILES])
        gate_sb = sb("gate_sb", [P, E])
        w1s = sb("w1s", [P, E, 2, F], F32R)
        w2s = sb("w2s", [P, E, FC, 2 * D], F32R)
        wqs = sb("wqs", [P, 2, H * DH], F32R)
        wks = sb("wks", [P, 2, P], F32R)
        wvs = sb("wvs", [P, 2, DH], F32R)
        wo_sb = sb("wo_sb", [P, H * DH // P, D])
        bout_sb = sb("bout_sb", [P, D])
        bias_tab = sb("bias_tab", [P, H, SEQ])
        stats = sb("stats", [P, TILES, 6])
        lnt = sb("lnt", [P, 6, TILES])
        mean = sb("mean", [P, TILES])
        rstd = sb("rstd", [P, TILES])
        gw1 = sb("gw1", [P, TILES])
        gw2 = sb("gw2", [P, TILES])
        eps_t = sb("eps_t", [P, 1])
        base = nc.sbuf_base

        raw1 = bias_tab[:, 0:E, :]
        raw2 = bias_tab[:, E:2 * E, :].rearrange("p e (c d) -> p e c d", c=FC)

        ffn = ExitStack()
        with ffn:
            def fb(name, shape, dt=F32):
                return ffn.enter_context(nc.sbuf_tensor(name, shape, dt))

            xng = fb("xng", [P, 2, 4, D])
            xngT = fb("xngT", [P, 2, 4 * P])
            lg = fb("lg", [P, TILES, E])
            lg2 = fb("lg2", [P, TILES, E])
            eq = fb("eq", [P, TILES, E])
            oh = fb("oh", [P, TOPK, TILES, E])
            ohb = fb("ohb", [P, TILES, E], BF16)
            top = fb("top", [P, 4, TILES])
            scan = fb("scan", [P, 2, 16 + TILES, E])
            cnt = fb("cnt", [P, E])
            cnti = fb("cnti", [P, E], I32)
            padded = fb("padded", [P, E])
            escan = fb("escan", [P, 2, 4 + E])
            ends = fb("ends", [P, E])
            place = fb("place", [P, TILES, E])
            pos = fb("pos", [P, PAIRS])
            posi = fb("posi", [P, 2, PAIRS], I32)
            posf = fb("posf", [P, 2, PAIRS])
            in_tile = fb("in_tile", [P, PAIRS, P], BF16)
            which = fb("which", [P, PAIRS, 2, ETILES], BF16)
            inv = fb("inv", [P, 2, ETILES])
            invt = fb("invt", [P, 2, ETILES])
            sidx = fb("sidx", [P, ETILES], I32)
            gidx = fb("gidx", [P, ETILES], I32)
            etf = fb("etf", [P, ETILES])
            etile = fb("etile", [P, ETILES], I32)
            wtmp = fb("wtmp", [P, 2, TILES])
            ecmp = in_tile[:, 0:ETILES // 2, :].bitcast(F32).rearrange("p a b -> p (a b)")[:, 0:ETILES * E].rearrange("p (t e) -> p t e", e=E)
            gring = fb("gring", [P, 4], I32)
            sring = fb("sring", [P, 4], I32)
            xr = fb("xr", [P, 4, D])
            xh = fb("xh", [P, 2, P], F32R)
            xl = fb("xl", [P, 2, P], F32R)
            hg = fb("hg", [P, 2, F])
            hh = fb("hh", [P, 2, F], F32R)
            hl = fb("hl", [P, 2, F], F32R)
            yt = fb("yt", [P, 2, D])
            yo = fb("yo", [P, 4, D])
            yc = in_tile[:, 0:PAIRS // 2, :].bitcast(F32).rearrange("p a b -> p (a b)").rearrange(
                "p (u q d) -> p u q d", u=2, q=4)
            rawq = which[:, 0:28, :, :].bitcast(F32).rearrange("p a b c -> p (a b c)")[:, 0:H * DH]
            rawkv = fb("rawkv", [P, 2 * DH])
            embT = fb("embT", [H, BUCKETS])
            brow = hg[0:H, :, :].rearrange("p a f -> p (a f)")[:, 0:SEQ + P]
        att = ExitStack()
        with att:
            def ab(name, shape, dt=F32):
                return att.enter_context(nc.sbuf_tensor(name, shape, dt))

            xa = ab("xa", [P, QT, D])
            xTh = ab("xTh", [P, SEQ], F32R)
            xTl = ab("xTl", [P, SEQ], F32R)
            kst = ab("kst", [P, 2, SEQ], F32R)
            vst = ab("vst", [P, QT, 2 * DH], F32R)
            qst = ab("qst", [P, 2, HG, SEQ], F32R)
            negs = ab("negs", [P, 4, SEQ])
            negmax = ab("negmax", [P, 8])
            prob = ab("prob", [P, 2, HG, SEQ])
            lsum = ab("lsum", [P, 2, HG])
            rsum = ab("rsum", [P, 2, HG])
            ph = ab("ph", [P, 2, HG * P], F32R)
            pl = ab("pl", [P, 2, HG * P], F32R)
            otl = ab("otl", [DH, 2, HG * P])
            ot = ab("ot", [P, 2, HG // 2, SEQ])

        bank = [ctx.enter_context(nc.psum_tensor(f"bank{i}", [P, 512], F32)) for i in range(8)]

        x_in = [sem(f"x_in{i}") for i in range(4)]
        w1_in, w2_in, wa_in, small_in = sem("w1_in"), sem("w2_in"), sem("wa_in"), sem("small_in")
        const_done, split_hi, split_lo = sem("const_done"), sem("split_hi"), sem("split_lo")
        brow_done, brow_out, bias_in = sem("brow_done"), sem("brow_out"), sem("bias_in")
        dstep = sem("dstep")
        vstep = [0]
        ln_ln = sem("ln_ln")
        ln_var = sem("ln_var")
        ln_done = sem("ln_done")
        xn_done, xnT_ps, xnT_sb, logit_ps = (sem(n) for n in ("xn_done", "xnT_ps", "xnT_sb", "logit_ps"))
        xn_out = [sem(f"xn_out{i}") for i in range(2)]
        gathered = [sem(f"gathered{i}") for i in range(4)]
        scattered = [sem(f"scattered{i}") for i in range(4)]
        lg_diff, lg_exp, hot_done, prefix_ps, onehot_done, inv_ps, route_done = (
            sem(n) for n in ("lg_diff", "lg_exp", "hot_done", "prefix_ps", "onehot_done", "inv_ps", "route_done"))
        gring_done, xrT_ps, xh_done, xl_done, up_ps, gelu_done, hT_ps, hh_done, hl_done, y_ps, yt_done, yo_done = (
            sem(n) for n in ("gring_done", "xrT_ps", "xh_done", "xl_done", "up_ps", "gelu_done", "hT_ps",
                             "hh_done", "hl_done", "y_ps", "yt_done", "yo_done"))
        y2_in = [sem("y2_in0"), sem("y2_in1")]
        comb1, combined, out_done = sem("comb1"), sem("combined"), sem("out_done")
        xa_done, misc_ps, misc_hi, misc_free, q_done, s_ps, s_done, exp_done, rsum_done, norm_done = (
            sem(n) for n in ("xa_done", "misc_ps", "misc_hi", "misc_free", "q_done", "s_ps", "s_done", "exp_done",
                             "rsum_done", "norm_done"))
        pt_ps, ph_done, pl_done, av_ps, otl_done, ot_done = (
            sem(n) for n in ("pt_ps", "ph_done", "pl_done", "av_ps", "otl_done", "ot_done"))

        block = ctx.enter_context(nc.Block())

        LAST = ETILES + 6
        MAIN0 = 8
        assert (ETILES - MAIN0) % 4 == 0

        def expert_steps(eng, step):
            for k in range(MAIN0):
                step(k, k, 0)
            with eng.Fori(0, (ETILES - MAIN0) // 4) as i:
                for u in range(4):
                    step(i * 4 + (MAIN0 + u), MAIN0 + u, i, loop=True)
            for k in range(ETILES, LAST):
                step(k, k, 0)

        carriers = {}

        def apart(eng):
            eng.reg_alu(carriers[eng], carriers[eng], 1, op=ALU.bitwise_and)

        def carrier(eng):
            carriers[eng] = eng.alloc_register("carrier")
            eng.reg_mov(carriers[eng], 1)

        def carried(eng):
            eng.wait_ge(const_done, carriers[eng])

        def dmas(r, i, s):
            return (i + (r * ETILES // 4 + s // 4 + 1)) * 16

        def on(k, lag, loop):
            return loop or 0 <= k - lag < ETILES

        def attention_plan():
            plan = [("xT",), ("K",), ("V",), ("Q", 0, 0), ("Q", 0, 1)]
            plan += [("S", 0, h) for h in range(HG)] + [("norm", 0)]
            for n in range(NG * QT):
                g, t = divmod(n, QT)
                a = [("S", n + 1, h) for h in range(HG)] + [("norm", n + 1)] if n + 1 < NG * QT else []
                b = []
                for jj in range(t + 2):
                    if jj <= t:
                        b.append(("T", n, jj))
                    if jj >= 1:
                        b.append(("AV", n, jj - 1))
                b.append(("O", n))
                if t == 2 and g + 1 < NG:
                    b = [("Q", g + 1, 0), ("Q", g + 1, 1)] + b
                if t == 1 and g >= 1:
                    b.append(("Y", g - 1))
                mix, na, nb = [], len(a), len(b)
                ia = ib = 0
                while ia < na or ib < nb:
                    if ib >= nb or (ia < na and ia * nb <= ib * na):
                        mix.append(a[ia])
                        ia += 1
                    else:
                        mix.append(b[ib])
                        ib += 1
                if t == 2 and g + 1 < NG:
                    mix = [m for m in mix if m[0] == "Q"] + [m for m in mix if m[0] != "Q"]
                plan += mix
            plan.append(("Y", NG - 1))
            return plan

        PLAN = attention_plan()
        MISC = [m for m in PLAN if m[0] in ("xT", "K", "V", "Q", "Y")]
        NM = len(MISC)
        NS = NG * QT * HG
        NU = NG * QT
        NB = NG * QT * (QT + 1) // 2

        def blk(n, jj):
            g, t = divmod(n, QT)
            return g * (QT * (QT + 1) // 2) + t * (t + 1) // 2 + jj

        S_BANK = [bank[0], bank[1], bank[2]]
        PT_BANK = [bank[3], bank[4]]
        OT_BANK = [bank[5], bank[6]]
        MB = bank[7]

        @block.sync
        def _(sp):
            xt = x.rearrange("b (t p) d -> p (b t) d", p=P)
            sp.dma_start(x_sb[:, 0:8, :], xt[:, 0:8, :]).then_inc(x_in[0], 16)
            sp.dma_start(gate_sb[:], gate_w).then_inc(small_in, 16)
            for i in range(1, 4):
                sp.dma_start(x_sb[:, 8 * i:8 * i + 8, :], xt[:, 8 * i:8 * i + 8, :]).then_inc(x_in[i], 16)
            sp.dma_start(raw1, fc_w.rearrange("e d f -> d e f")).then_inc(w1_in, 16)
            sp.dma_start(raw2, proj_w.rearrange("e (c p) d -> p e c d", p=P)).then_inc(w2_in, 16)
            sp.wait_ge(brow_done, 1)
            sp.dma_start(bias_dram, brow.unsqueeze(1).to_broadcast([H, P, ROW])).then_inc(brow_out, 16)
            sp.wait_ge(brow_out, 16)
            sp.wait_ge(split_lo, 2)
            src = bass.AP(tensor=bias_dram.tensor, offset=bias_dram.offset + P - 1,
                          ap=[[ROW - 1, P], [P * ROW, H], [1, SEQ]])
            sp.dma_start(bias_tab[:], src).then_inc(bias_in, 16)

            def ffn_sp(r):
                xd = xn_dram[r].rearrange("(t p) d -> p t d", p=P)
                with sp.Fori(0, TILES // 8) as i:
                    for u in range(2):
                        gi = i * 2 + u
                        sp.wait_ge(xn_done, r * TILES + gi * 4 + 4)
                        sp.dma_start(xd[:, ds(gi * 4, 4), :], xng[:, u, :, :]).then_inc(xn_out[u], 16)
                for s in range(4):
                    sp.wait_ge(scattered[s], 4 * ETILES * (r + 1))
                yd = y2_dram[r].rearrange("(t p k) d -> p t (k d)", p=P, k=TOPK)
                for gi in range(2):
                    sp.dma_start(yc[:, gi, :, :], yd[:, 4 * gi:4 * gi + 4, :]).then_inc(y2_in[gi], 16)
                with sp.Fori(1, TILES // 8) as i:
                    for u in range(2):
                        gi = i * 2 + u
                        sp.wait_ge(combined, r * TILES + gi * 4 - 4)
                        sp.dma_start(yc[:, u, :, :], yd[:, ds(gi * 4, 4), :]).then_inc(y2_in[u], 16)

            ffn_sp(0)
            if stop > 1:
                ffn_sp(1)
            ot_ = out.rearrange("b (t p) d -> p (b t) d", p=P)
            sp.wait_ge(combined if stop != 1 else misc_free, (2 if stop > 1 else 1) * TILES if stop != 1 else BATCH * NM)
            sp.dma_start(ot_, x_sb[:]).then_inc(out_done, 16)
            sp.wait_ge(out_done, 16)

        @block.gpsimd
        def _(gp):
            g = nc.gpsimd
            carrier(gp)
            g.memset(ident[:], 0.0).then_inc(const_done, 1)
            g.memset(before[:], 1.0).then_inc(const_done, 1)
            g.memset(ones_bf[:], 1.0).then_inc(const_done, 1)
            gp.wait_ge(const_done, 3)
            g.affine_select(out=ident[:], in_=ident[:], compare_op=ALU.not_equal, fill=1.0,
                            base=0, pattern=[[-1, P]], channel_multiplier=1).then_inc(const_done, 1)
            g.affine_select(out=before[:], in_=before[:], compare_op=ALU.is_gt, fill=0.0,
                            base=0, pattern=[[1, P]], channel_multiplier=-1).then_inc(const_done, 1)
            iota = dict(allow_small_or_imprecise_dtypes=True)
            g.iota(iota_p[:], pattern=[[1, P]], base=0, channel_multiplier=0, **iota).then_inc(const_done, 1)
            g.iota(pair_val[:], pattern=[[1, TOPK]], base=1, channel_multiplier=2, **iota).then_inc(const_done, 1)
            g.iota(tile_val[:], pattern=[[0, TOPK], [1, TILES]], base=0, channel_multiplier=0, **iota).then_inc(const_done, 1)
            g.iota(rev8[:], pattern=[[-1, E]], base=E, channel_multiplier=0, **iota).then_inc(const_done, 1)
            g.iota(tile_start[:], pattern=[[P, ETILES]], base=0, channel_multiplier=0, **iota).then_inc(const_done, 1)
            g.memset(eps_t[:], EPS).then_inc(const_done, 1)
            g.memset(scan[:, :, 0:17, :], 0.0).then_inc(const_done, 1)
            g.memset(escan[:, :, 0:5], 0.0).then_inc(const_done, 1)
            g.dma_start(rawq, Wq).then_inc(wa_in, 16)
            g.dma_start(rawkv[:], Wkv).then_inc(wa_in, 16)
            g.dma_start(wo_sb[:], Wout.rearrange("(c p) d -> p c d", p=P)).then_inc(wa_in, 16)
            g.dma_start(embT[:], rel_emb.rearrange("k h -> h k"), allow_slow_non_contiguous=True).then_inc(wa_in, 16)
            g.dma_start(bout_sb[:], bout.rearrange("(a d) -> a d", a=1).to_broadcast([P, D])).then_inc(wa_in, 16)

            def ffn_pool(r):
                k0 = r * ETILES
                if r:
                    gp.wait_ge(misc_free, BATCH * NM)
                    g.memset(scan[:, :, 0:17, :], 0.0).then_inc(const_done, 1)
                    g.memset(escan[:, :, 0:5], 0.0).then_inc(const_done, 1)
                gp.wait_ge(route_done, r + 1)
                for u in range(2):
                    gp.wait_ge(xn_out[u], 16 * (TILES // 8) * (r + 1))

                def step(k, s, i, loop=False):
                    if on(k, 0, loop):
                        gp.wait_ge(gring_done, k0 + k + 1)
                        if loop or k >= 4:
                            gp.wait_ge(xrT_ps, k0 + k - 3)
                        apart(gp)
                        g.indirect_dma_start(out=xr[:, s % 4, :], out_offset=None, in_=xn_dram[r],
                                             in_offset=bass.IndirectOffsetOnAxis(ap=gring[:, s % 4:s % 4 + 1], axis=0),
                                             ).then_inc(gathered[s % 4], 16)
                    if on(k, 6, loop):
                        gp.wait_ge(yo_done, k0 + k - 5)
                        q = (s - 6) % 4
                        apart(gp)
                        g.indirect_dma_start(out=y2_dram[r], in_=yo[:, q, :], in_offset=None,
                                             out_offset=bass.IndirectOffsetOnAxis(ap=sring[:, q:q + 1], axis=0),
                                             bounds_check=TILES * P * TOPK - 1, oob_is_err=False).then_inc(scattered[q], 16)

                expert_steps(gp, step)

            ffn_pool(0)
            if stop > 0:
                with gp.Fori(0, BATCH) as b:
                    for task in PLAN:
                        if task[0] == "norm":
                            n = task[1]
                            w = (n % QT + 1) * P
                            gp.wait_ge(rsum_done, b * NU + (n + 1))
                            pv = prob[:, n % 2, :, 0:w]
                            g.tensor_tensor(out=pv, in0=pv, in1=rsum[:, n % 2, :].unsqueeze(2).to_broadcast([P, HG, w]),
                                            op=ALU.mult).then_inc(norm_done, 1)
            if stop > 1:
                ffn_pool(1)
            carried(gp)

        @block.scalar
        def _(act):
            a = nc.scalar
            act.wait_ge(w1_in, 16)
            a.activation(w1s[:, :, 0, :], raw1, ACT.Copy).then_inc(split_hi, 1)
            act.wait_ge(w2_in, 16)
            a.activation(w2s[:, :, :, 0:D], raw2, ACT.Copy).then_inc(split_hi, 1)
            act.wait_ge(wa_in, 80)
            a.activation(wqs[:, 0, :], rawq, ACT.Copy).then_inc(split_hi, 1)
            a.activation(wks[:, 0, 0:DH], rawkv[:, 0:DH], ACT.Copy).then_inc(split_hi, 1)
            a.activation(wks[:, 0, DH:P], rawkv[:, 0:DH], ACT.Copy).then_inc(split_hi, 1)
            a.activation(wvs[:, 0, :], rawkv[:, DH:P], ACT.Copy).then_inc(split_hi, 1)

            def ln_act(r):
                act.wait_ge(const_done, 13)
                act.wait_ge(ln_var, r + 1)
                a.activation(lnt[:, 3, :], lnt[:, 2, :], ACT.Ln, bias=eps_t[:, 0:1]).then_inc(ln_ln, 1)
                act.wait_ge(ln_ln, 2 * r + 1)
                a.activation(lnt[:, 4, :], lnt[:, 3, :], ACT.Exp, scale=-0.5).then_inc(ln_ln, 1)

            def ffn_act(r):
                ln_act(2 * r)
                with act.Fori(0, TILES // 8) as i:
                    for u in range(2):
                        act.wait_ge(xnT_ps, r * (TILES // 4) + i * 2 + (u + 1))
                        a.activation(xngT[:, u, :], bank[u][:], ACT.Copy).then_inc(xnT_sb, 1)
                act.wait_ge(lg_diff, r + 1)
                a.activation(wtmp[:, 1, :], wtmp[:, 0, :], ACT.Exp).then_inc(lg_exp, 1)
                k0 = r * ETILES

                def step(k, s, i, loop=False):
                    if on(k, 2, loop):
                        q = (s - 2) % 2
                        act.wait_ge(xrT_ps, k0 + k - 1)
                        if loop or k >= 4:
                            act.wait_ge(up_ps, k0 + k - 3)
                        a.activation(xh[:, q, :], bank[q][:, 0:P], ACT.Copy).then_inc(xh_done, 1)
                    if on(k, 3, loop):
                        q = (s - 3) % 2
                        act.wait_ge(up_ps, k0 + k - 2)
                        if loop or k >= 5:
                            act.wait_ge(hT_ps, k0 + k - 4)
                        a.activation(hg[:, q, :], bank[2 + q][:], ACT.Gelu).then_inc(gelu_done, 1)
                    if on(k, 4, loop):
                        q = (s - 4) % 2
                        act.wait_ge(hT_ps, k0 + k - 3)
                        if loop or k >= 6:
                            act.wait_ge(y_ps, k0 + k - 5)
                        a.activation(hh[:, q, :], bank[4 + q][:], ACT.Copy).then_inc(hh_done, 1)
                    if on(k, 5, loop):
                        q = (s - 5) % 2
                        act.wait_ge(y_ps, k0 + k - 4)
                        if loop or k >= 7:
                            act.wait_ge(yo_done, k0 + k - 6)
                        a.activation(yt[:, q, :], bank[6 + q][:, D:2 * D], ACT.Copy).then_inc(yt_done, 1)

                expert_steps(act, step)

            def attention_act(b):
                m = 0
                for task in PLAN:
                    kind = task[0]
                    if kind in ("xT", "K", "V"):
                        act.wait_ge(misc_ps, b * NM + (m + 1))
                        dst = {"xT": xTh[:], "K": kst[:, 0, :], "V": vst[:, :, 0:DH]}[kind]
                        src = MB[:, 0:QT * DH].rearrange("p (t d) -> p t d", d=DH) if kind == "V" else MB[:]
                        a.activation(dst, src, ACT.Copy).then_inc(misc_hi, 1)
                        m += 1
                    elif kind == "Q":
                        _, g, c = task
                        act.wait_ge(misc_ps, b * NM + (m + 1))
                        if g >= 2 and c == 0:
                            act.wait_ge(s_ps, b * NS + (g - 1) * QT * HG)
                        for o in range(2):
                            a.activation(qst[0:DH, g % 2, 2 * c + o, :], MB[DH * o:DH * o + DH, :], ACT.Copy,
                                         scale=DH ** -0.5).then_inc(misc_hi, 1)
                        m += 1
                    elif kind == "Y":
                        m += 1
                    elif kind == "S":
                        _, n, h = task
                        w = (n % QT + 1) * P
                        act.wait_ge(s_done, b * NS + (HG * n + h + 1))
                        if n >= 2 and h == 0:
                            act.wait_ge(pt_ps, b * NB + blk(n - 2, (n - 2) % QT) + 1)
                        a.activation(prob[:, n % 2, h, 0:w], negs[:, h, 0:w], ACT.Exp, scale=-1.0,
                                     bias=negmax[:, (HG * n + h) % 8:(HG * n + h) % 8 + 1],
                                     accum_out=lsum[:, n % 2, h:h + 1]).then_inc(exp_done, 1)
                    elif kind == "T":
                        _, n, jj = task
                        i = blk(n, jj)
                        act.wait_ge(pt_ps, b * NB + (i + 1))
                        if i >= 2:
                            act.wait_ge(av_ps, b * NB + (i - 1))
                        a.activation(ph[:, i % 2, :], PT_BANK[i % 2][:], ACT.Copy).then_inc(ph_done, 1)
                    elif kind == "O":
                        n = task[1]
                        act.wait_ge(av_ps, b * NB + blk(n, n % QT) + 1)
                        if n >= 2:
                            act.wait_ge(ot_done, b * NU + (n - 1))
                        a.activation(otl[:, n % 2, :], OT_BANK[n % 2][DH:P, :], ACT.Copy).then_inc(otl_done, 1)

            ffn_act(0)
            if stop > 0:
                ln_act(1)
                with act.Fori(0, BATCH) as b:
                    attention_act(b)
            if stop > 1:
                ffn_act(1)

        @block.vector
        def _(dve):
            v = nc.vector
            carrier(dve)

            def step_done(ins):
                vstep[0] += 1
                ins.then_inc(dstep, 1)
                dve.wait_ge(dstep, vstep[0])

            def async_done(ins):
                vstep[0] += 1
                ins.then_inc(dstep, 1)

            def waited():
                dve.wait_ge(dstep, vstep[0])

            def layer_norm_stats(r, first=False):
                if first:
                    for c in range(4):
                        dve.wait_ge(x_in[c], 16)
                with dve.Fori(0, TILES) as i:
                    v.bn_stats(out=stats[:, ds(i, 1), :].rearrange("p a s -> p (a s)"),
                               in_=x_sb[:, ds(i, 1), :].rearrange("p a d -> p (a d)")).then_inc(dstep, 1)
                vstep[0] += TILES
                waited()
                me, m2e, mo, m2o = (stats[:, :, s] for s in (1, 2, 4, 5))
                async_done(v.tensor_tensor(lnt[:, 0, :], me, mo, ALU.add))
                async_done(v.tensor_tensor(lnt[:, 1, :], me, mo, ALU.subtract))
                async_done(v.tensor_tensor(lnt[:, 5, :], m2e, m2o, ALU.add))
                waited()
                async_done(v.tensor_scalar(mean[:], lnt[:, 0, :], 0.5, None, ALU.mult))
                step_done(v.scalar_tensor_tensor(out=lnt[:, 3, :], in0=lnt[:, 1, :], scalar=D / 4.0, in1=lnt[:, 1, :],
                                                 op0=ALU.mult, op1=ALU.mult))
                step_done(v.tensor_tensor(lnt[:, 5, :], lnt[:, 5, :], lnt[:, 3, :], ALU.add))
                v.tensor_scalar(lnt[:, 2, :], lnt[:, 5, :], 1.0 / D, None, ALU.mult).then_inc(ln_var, 1)
                dve.wait_ge(ln_ln, 2 * r + 2)
                y = lnt[:, 4, :]
                step_done(v.tensor_tensor(lnt[:, 0, :], y, y, ALU.mult))
                step_done(v.scalar_tensor_tensor(out=lnt[:, 1, :], in0=lnt[:, 2, :], scalar=EPS, in1=lnt[:, 0, :],
                                                 op0=ALU.add, op1=ALU.mult))
                step_done(v.tensor_scalar(lnt[:, 0, :], lnt[:, 1, :], -0.5, 1.5, ALU.mult, ALU.add))
                step_done(v.tensor_tensor(rstd[:], y, lnt[:, 0, :], ALU.mult))

            def routing(r):
                bc = lambda t: t.unsqueeze(2).to_broadcast([P, TILES, E])
                dve.wait_ge(logit_ps, (r + 1) * TILES)
                if r:
                    carried(dve)
                step_done(v.tensor_copy(lg[:].rearrange("p t e -> p (t e)"), bank[2][:, 0:TILES * E]))
                rev = rev8[:].unsqueeze(1).to_broadcast([P, TILES, E])
                src = lg
                for c in range(TOPK):
                    step_done(v.tensor_reduce(out=top[:, c, :], in_=src[:], op=ALU.max, axis=AX))
                    step_done(v.tensor_tensor(eq[:], src[:], bc(top[:, c, :]), ALU.is_equal))
                    step_done(v.tensor_tensor(eq[:], eq[:], rev, ALU.mult))
                    step_done(v.tensor_reduce(out=top[:, 2 + c, :], in_=eq[:], op=ALU.max, axis=AX))
                    step_done(v.tensor_tensor(oh[:, c, :, :], rev, bc(top[:, 2 + c, :]), ALU.is_equal))
                    if c == 0:
                        step_done(v.scalar_tensor_tensor(out=lg2[:], in0=oh[:, 0, :, :], scalar=MASKED, in1=lg[:],
                                                         op0=ALU.mult, op1=ALU.add))
                        src = lg2
                v.tensor_tensor(ohb[:], oh[:, 0, :, :], oh[:, 1, :, :], ALU.add).then_inc(hot_done, 1)
                v.tensor_tensor(wtmp[:, 0, :], top[:, 1, :], top[:, 0, :], ALU.subtract).then_inc(lg_diff, 1)
                dve.wait_ge(prefix_ps, r + 1)
                if r:
                    dve.wait_ge(const_done, 15)
                tot = bank[3][:, 0:TILES * E].rearrange("p (t e) -> p t e", e=E)
                step_done(v.tensor_copy(scan[:, 0, 17:16 + TILES, :], tot[:, 0:TILES - 1, :]))
                cur = 0
                for sh in (1, 2, 4, 8, 16):
                    step_done(v.tensor_tensor(scan[:, 1 - cur, 16:, :], scan[:, cur, 16:, :],
                                              scan[:, cur, 16 - sh:16 + TILES - sh, :], ALU.add))
                    cur = 1 - cur
                step_done(v.tensor_tensor(cnt[:], scan[:, cur, 15 + TILES, :], tot[:, TILES - 1, :], ALU.add))
                step_done(v.tensor_scalar(cnti[:], cnt[:], float(P - 1), None, ALU.add))
                step_done(v.tensor_scalar(cnti[:], cnti[:], 7, 7, ALU.logical_shift_right, ALU.logical_shift_left))
                async_done(v.tensor_copy(padded[:], cnti[:]))
                step_done(v.tensor_copy(escan[:, 0, 5:4 + E], cnti[:, 0:E - 1]))
                ec = 0
                for sh in (1, 2, 4):
                    step_done(v.tensor_tensor(escan[:, 1 - ec, 4:], escan[:, ec, 4:], escan[:, ec, 4 - sh:4 + E - sh], ALU.add))
                    ec = 1 - ec
                ebase = escan[:, ec, 4:]
                async_done(v.tensor_tensor(ends[:], ebase, padded[:], ALU.add))
                step_done(v.tensor_tensor(place[:], scan[:, cur, 16:, :], ebase.unsqueeze(1).to_broadcast([P, TILES, E]), ALU.add))
                step_done(v.tensor_tensor(place[:], place[:], bank[4][:, 0:TILES * E].rearrange("p (t e) -> p t e", e=E), ALU.add))
                for c in range(TOPK):
                    step_done(v.tensor_tensor(eq[:], place[:], oh[:, c, :, :], ALU.mult))
                    step_done(v.tensor_reduce(out=pos[:, c * TILES:(c + 1) * TILES], in_=eq[:], op=ALU.add, axis=AX))
                step_done(v.tensor_copy(posi[:, 0, :], pos[:]))
                async_done(v.tensor_scalar(posi[:, 1, :], posi[:, 0, :], 7, None, ALU.logical_shift_right))
                waited()
                step_done(v.tensor_scalar(posi[:, 0, :], posi[:, 0, :], P - 1, None, ALU.bitwise_and))
                step_done(v.tensor_copy(posf[:], posi[:]))
                step_done(v.tensor_tensor(ecmp, tile_start[:].unsqueeze(2).to_broadcast([P, ETILES, E]),
                                          ends[:].unsqueeze(1).to_broadcast([P, ETILES, E]), ALU.is_ge))
                step_done(v.tensor_reduce(out=etf[:], in_=ecmp[:, :, 0:E - 1], op=ALU.add, axis=AX))
                async_done(v.tensor_copy(etile[:], etf[:]))
                async_done(v.tensor_tensor(in_tile[:], iota_p[:].unsqueeze(1).to_broadcast([P, PAIRS, P]),
                                           posf[:, 0, :].unsqueeze(2).to_broadcast([P, PAIRS, P]), ALU.is_equal))
                step_done(v.tensor_tensor(posf[:, 1, :], pos[:], posf[:, 0, :], ALU.subtract))
                ts = tile_start[:].unsqueeze(1).to_broadcast([P, PAIRS, ETILES])
                step_done(v.tensor_tensor(which[:, :, 0, :], ts, posf[:, 1, :].unsqueeze(2).to_broadcast([P, PAIRS, ETILES]), ALU.is_equal))
                async_done(v.tensor_tensor(which[:, :, 1, :], which[:, :, 0, :],
                                           tile_val[:].unsqueeze(2).to_broadcast([P, PAIRS, ETILES]), ALU.mult))
                waited()
                for c in range(TOPK):
                    last = v.tensor_scalar(which[:, c * TILES:(c + 1) * TILES, 0, :], which[:, c * TILES:(c + 1) * TILES, 0, :],
                                           pair_val[:, c:c + 1], None, ALU.mult)
                    if c < TOPK - 1:
                        async_done(last)
                last.then_inc(onehot_done, 1)
                dve.wait_ge(lg_exp, r + 1)
                step_done(v.tensor_scalar(wtmp[:, 0, :], wtmp[:, 1, :], 2.0, 2.0, ALU.mult, ALU.add))
                step_done(v.reciprocal(gw1[:], wtmp[:, 0, :]))
                step_done(v.tensor_tensor(gw2[:], gw1[:], wtmp[:, 1, :], ALU.mult))
                dve.wait_ge(inv_ps, r + 1)
                step_done(v.tensor_copy(inv[:].rearrange("p a b -> p (a b)"), bank[5][:, 0:2 * ETILES]))
                step_done(v.scalar_tensor_tensor(out=invt[:, 0, :], in0=inv[:, 1, :], scalar=2.0 * P, in1=inv[:, 0, :],
                                                 op0=ALU.mult, op1=ALU.add))
                step_done(v.tensor_scalar(invt[:, 1, :], invt[:, 0, :], 0.0, 1.0e5, ALU.is_equal, ALU.mult))
                step_done(v.scalar_tensor_tensor(out=inv[:, 0, :], in0=invt[:, 0, :], scalar=-1.0, in1=invt[:, 1, :],
                                                 op0=ALU.add, op1=ALU.add))
                step_done(v.tensor_copy(sidx[:], inv[:, 0, :]))
                step_done(v.tensor_scalar(invt[:, 1, :], invt[:, 0, :], -1.0, 0.0, ALU.add, ALU.max))
                step_done(v.tensor_copy(gidx[:], invt[:, 1, :]))
                v.tensor_scalar(gidx[:], gidx[:], 1, None, ALU.logical_shift_right).then_inc(route_done, 1)
                dve.wait_ge(route_done, r + 1)

            def ffn_dve(r):
                layer_norm_stats(2 * r, first=(r == 0))
                if r == 0:
                    dve.wait_ge(const_done, 13)
                g0 = r * (TILES // 4)

                def norm_group(gi, u):
                    for q in range(4):
                        t = gi * 4 + q
                        v.tensor_scalar(xng[:, u, q, :], x_sb[:, ds(t, 1), :].rearrange("p a d -> p (a d)"),
                                        mean[:, ds(t, 1)], rstd[:, ds(t, 1)], ALU.subtract, ALU.mult).then_inc(xn_done, 1)

                for u in range(2):
                    norm_group(u, u)
                with dve.Fori(1, TILES // 8) as i:
                    for u in range(2):
                        gi = i * 2 + u
                        dve.wait_ge(xnT_ps, g0 + gi - 1)
                        dve.wait_ge(xn_out[u], (i + r * (TILES // 8)) * 16)
                        norm_group(gi, u)
                routing(r)
                k0 = r * ETILES

                def step(k, s, i, loop=False):
                    if on(k, 0, loop):
                        if loop or k >= 4:
                            dve.wait_ge(gathered[s % 4], dmas(r, i, s - 4))
                        v.tensor_copy(gring[:, s % 4:s % 4 + 1], gidx[:, ds(k, 1)]).then_inc(gring_done, 1)
                    if on(k, 2, loop):
                        q = (s - 2) % 2
                        dve.wait_ge(xh_done, k0 + k - 1)
                        v.tensor_tensor(xl[:, q, :], bank[q][:, 0:P], xh[:, q, :].bitcast(F32), ALU.subtract).then_inc(xl_done, 1)
                    if on(k, 4, loop):
                        q = (s - 4) % 2
                        dve.wait_ge(hh_done, k0 + k - 3)
                        v.tensor_tensor(hl[:, q, :], bank[4 + q][:], hh[:, q, :].bitcast(F32), ALU.subtract).then_inc(hl_done, 1)
                    if on(k, 5, loop):
                        q = (s - 5) % 2
                        dve.wait_ge(yt_done, k0 + k - 4)
                        if loop or k >= 9:
                            dve.wait_ge(scattered[(s - 5) % 4], dmas(r, i, s - 9))
                        v.tensor_copy(sring[:, (s - 5) % 4:(s - 5) % 4 + 1], sidx[:, ds(k - 5, 1)])
                        v.tensor_tensor(yo[:, (s - 5) % 4, :], bank[6 + q][:, 0:D], yt[:, q, :], ALU.add).then_inc(yo_done, 1)

                expert_steps(dve, step)
                for gi in range(2):
                    combine(r, gi, gi, 1)
                with dve.Fori(1, TILES // 8) as i:
                    for u in range(2):
                        combine(r, i * 2 + u, u, i + 1)

            def combine(r, gi, u, nth):
                dve.wait_ge(y2_in[u], (r * (TILES // 8) + nth) * 16)
                for c, w in ((0, gw1), (1, gw2)):
                    for q in range(4):
                        t = gi * 4 + q
                        xt = x_sb[:, ds(t, 1), :].rearrange("p a d -> p (a d)")
                        ins = v.scalar_tensor_tensor(out=xt, in0=yc[:, u, q, c * D:(c + 1) * D], scalar=w[:, ds(t, 1)],
                                                     in1=xt, op0=ALU.mult, op1=ALU.add)
                        ins.then_inc(comb1 if c == 0 else combined, 1)
                    if c == 0:
                        dve.wait_ge(comb1, r * TILES + gi * 4 + 4)

            def attention_dve(b):
                for q in range(QT):
                    t = b * QT + q
                    v.tensor_scalar(xa[:, q, :], x_sb[:, ds(t, 1), :].rearrange("p a d -> p (a d)"),
                                    mean[:, ds(t, 1)], rstd[:, ds(t, 1)], ALU.subtract, ALU.mult).then_inc(xa_done, 1)
                dve.wait_ge(xa_done, b * (QT + 1) + QT)
                xb = x_sb[:, ds(b * QT, QT), :]
                v.tensor_tensor(xb, xb, bout_sb[:].unsqueeze(1).to_broadcast([P, QT, D]), ALU.add).then_inc(xa_done, 1)
                m = hi = 0
                for task in PLAN:
                    kind = task[0]
                    if kind in ("xT", "K", "V"):
                        hi += 1
                        dve.wait_ge(misc_hi, b * (3 + H) + hi)
                        hi_t, dst = {"xT": (xTh[:], xTl[:]), "K": (kst[:, 0, :], kst[:, 1, :]),
                                     "V": (vst[:, :, 0:DH], vst[:, :, DH:])}[kind]
                        src = MB[:, 0:QT * DH].rearrange("p (t d) -> p t d", d=DH) if kind == "V" else MB[:]
                        v.tensor_tensor(dst, src, hi_t.bitcast(F32), ALU.subtract).then_inc(misc_free, 1)
                        m += 1
                    elif kind == "Q":
                        _, g, c = task
                        for o in range(2):
                            hi += 1
                            dve.wait_ge(misc_hi, b * (3 + H) + hi)
                            ins = v.scalar_tensor_tensor(out=qst[DH:P, g % 2, 2 * c + o, :], in0=MB[DH * o:DH * o + DH, :],
                                                         scalar=DH ** -0.5, in1=qst[0:DH, g % 2, 2 * c + o, :].bitcast(F32),
                                                         op0=ALU.mult, op1=ALU.subtract)
                        ins.then_inc(misc_free, 1)
                        m += 1
                    elif kind == "Y":
                        dve.wait_ge(misc_ps, b * NM + (m + 1))
                        dve.wait_ge(xa_done, (b + 1) * (QT + 1))
                        if task[1]:
                            dve.wait_ge(misc_free, b * NM + (MISC.index(("Y", task[1] - 1)) + 1))
                        v.tensor_tensor(xb, xb, MB[:].rearrange("p (t d) -> p t d", d=D), ALU.add).then_inc(misc_free, 1)
                        m += 1
                    elif kind == "S":
                        _, n, h = task
                        t, i = n % QT, HG * n + h
                        w = (t + 1) * P
                        dve.wait_ge(s_ps, b * NS + (i + 1))
                        if i >= 4:
                            dve.wait_ge(exp_done, b * NS + (i - 3))
                        apart(dve)
                        v.tensor_tensor_reduce(out=negs[:, h, 0:w], in0=S_BANK[i % 3][:, 0:w],
                                               in1=bias_tab[:, HG * (n // QT) + h, SEQ - w:SEQ], scale=-1.0, scalar=3.4e38,
                                               op0=ALU.add, op1=ALU.min,
                                               accum_out=negmax[:, i % 8:i % 8 + 1]).then_inc(s_done, 1)
                    elif kind == "norm":
                        n = task[1]
                        dve.wait_ge(exp_done, b * NS + HG * (n + 1))
                        v.reciprocal(rsum[:, n % 2, :], lsum[:, n % 2, :]).then_inc(rsum_done, 1)
                    elif kind == "T":
                        _, n, jj = task
                        i = blk(n, jj)
                        dve.wait_ge(ph_done, b * NB + (i + 1))
                        v.tensor_tensor(pl[:, i % 2, :], PT_BANK[i % 2][:], ph[:, i % 2, :].bitcast(F32),
                                        ALU.subtract).then_inc(pl_done, 1)
                    elif kind == "O":
                        n = task[1]
                        g, t = divmod(n, QT)
                        dve.wait_ge(otl_done, b * NU + (n + 1))
                        if g >= 2 and t == 0:
                            dve.wait_ge(misc_ps, b * NM + MISC.index(("Y", g - 2)) + 1)
                        for o in range(2):
                            sel = lambda z: z.rearrange("p (c o i) -> p o c i", o=2, i=P)[:, o, :, :]
                            ins = v.tensor_tensor(ot[DH * o:DH * o + DH, g % 2, :, t * P:(t + 1) * P],
                                                  sel(OT_BANK[n % 2][0:DH, :]), sel(otl[:, n % 2, :]), ALU.add)
                        ins.then_inc(ot_done, 1)

            dve.wait_ge(split_hi, 1)
            v.tensor_tensor(w1s[:, :, 1, :], raw1, w1s[:, :, 0, :].bitcast(F32), ALU.subtract).then_inc(split_lo, 1)
            dve.wait_ge(split_hi, 2)
            v.tensor_tensor(w2s[:, :, :, D:], raw2, w2s[:, :, :, 0:D].bitcast(F32), ALU.subtract).then_inc(split_lo, 1)
            dve.wait_ge(split_hi, 6)
            v.tensor_tensor(wqs[:, 1, :], rawq, wqs[:, 0, :].bitcast(F32), ALU.subtract).then_inc(split_lo, 1)
            for z in range(2):
                v.tensor_tensor(wks[:, 1, z * DH:(z + 1) * DH], rawkv[:, 0:DH], wks[:, 0, 0:DH].bitcast(F32), ALU.subtract).then_inc(split_lo, 1)
            v.tensor_tensor(wvs[:, 1, :], rawkv[:, DH:P], wvs[:, 0, :].bitcast(F32), ALU.subtract).then_inc(split_lo, 1)
            async_done(v.memset(brow[:, SEQ:], MASKED))
            for k, n0, n1 in bucket_runs():
                async_done(v.tensor_scalar(brow[:, SEQ - n1:SEQ - n0], embT[:, k:k + 1].to_broadcast([H, n1 - n0]),
                                           DH ** 0.5, None, ALU.mult))
            waited()
            v.engine_nop().then_inc(brow_done, 1)
            ffn_dve(0)
            if stop > 0:
                dve.wait_ge(combined, TILES)
                layer_norm_stats(1)
                dve.wait_ge(bias_in, 16)
                with dve.Fori(0, BATCH) as b:
                    attention_dve(b)
            if stop > 1:
                dve.wait_ge(misc_free, BATCH * NM)
                ffn_dve(1)

        @block.tensor
        def _(pe):
            t_ = nc.tensor
            pe.wait_ge(const_done, 13)
            pe.wait_ge(small_in, 16)

            def three(dst, hi, lo, mh, ml, first=True, last=True):
                t_.matmul(dst, hi, mh, start=first, stop=False)
                t_.matmul(dst, hi, ml, start=False, stop=False)
                return t_.matmul(dst, lo, mh, start=False, stop=last)

            def ffn_pe(r):
                g0 = r * (TILES // 4)
                with pe.Fori(0, TILES // 8) as i:
                    for u in range(2):
                        gi = i * 2 + u
                        pe.wait_ge(xn_done, r * TILES + gi * 4 + 4)
                        for q in range(4):
                            ins = t_.transpose(bank[u][:, q * P:(q + 1) * P], xng[:, u, q, :], ident[:])
                        ins.then_inc(xnT_ps, 1)
                        pe.wait_ge(xnT_sb, g0 + gi + 1)
                        for q in range(4):
                            t_.matmul(bank[2][:, ds((gi * 4 + q) * E, E)], xngT[:, u, q * P:(q + 1) * P], gate_sb[:],
                                      start=True, stop=True).then_inc(logit_ps, 1)
                pe.wait_ge(hot_done, r + 1)
                hot = ohb[:].rearrange("p t e -> p (t e)")
                t_.matmul(bank[3][:, 0:TILES * E], ones_bf[:], hot, start=True, stop=True)
                t_.matmul(bank[4][:, 0:TILES * E], before[:], hot, start=True, stop=True).then_inc(prefix_ps, 1)
                pe.wait_ge(onehot_done, r + 1)
                for c in range(PAIRS):
                    ins = t_.matmul(bank[5][:, 0:2 * ETILES], in_tile[:, c, :], which[:, c, :, :].rearrange("p a b -> p (a b)"),
                                    start=(c == 0), stop=(c == PAIRS - 1))
                ins.then_inc(inv_ps, 1)
                pe.wait_ge(route_done, r + 1)
                if r == 0:
                    pe.wait_ge(split_lo, 2)
                k0 = r * ETILES

                def step(k, s, i, loop=False):
                    if on(k, 2, loop):
                        q = (s - 2) % 2
                        pe.wait_ge(gathered[(s - 2) % 4], dmas(r, i, s - 2))
                        if loop or k >= 4:
                            pe.wait_ge(xl_done, k0 + k - 3)
                        t_.transpose(bank[q][:, 0:P], xr[:, (s - 2) % 4, :], ident[:]).then_inc(xrT_ps, 1)
                    if on(k, 3, loop):
                        q = (s - 3) % 2
                        e = pe.value_load(etile[0:1, ds(k - 3, 1)], min_val=0, max_val=E - 1)
                        pe.wait_ge(xl_done, k0 + k - 2)
                        if loop or k >= 5:
                            pe.wait_ge(gelu_done, k0 + k - 4)
                        wh, wl = (w1s[:, ds(e, 1), z, :].rearrange("p a f -> p (a f)") for z in range(2))
                        three(bank[2 + q][:], xh[:, q, :], xl[:, q, :], wh, wl).then_inc(up_ps, 1)
                    if on(k, 4, loop):
                        q = (s - 4) % 2
                        pe.wait_ge(gelu_done, k0 + k - 3)
                        if loop or k >= 6:
                            pe.wait_ge(hl_done, k0 + k - 5)
                        for c in range(FC):
                            ins = t_.transpose(bank[4 + q][:, c * P:(c + 1) * P], hg[:, q, c * P:(c + 1) * P], ident[:])
                        ins.then_inc(hT_ps, 1)
                    if on(k, 5, loop):
                        q = (s - 5) % 2
                        e = pe.value_load(etile[0:1, ds(k - 5, 1)], min_val=0, max_val=E - 1)
                        pe.wait_ge(hl_done, k0 + k - 4)
                        if loop or k >= 7:
                            pe.wait_ge(yo_done, k0 + k - 6)
                        for c in range(FC):
                            w = w2s[:, ds(e, 1), c, :].rearrange("p a d -> p (a d)")
                            t_.matmul(bank[6 + q][:, 0:2 * D], hh[:, q, c * P:(c + 1) * P], w, start=(c == 0), stop=False)
                            ins = t_.matmul(bank[6 + q][:, 0:2 * D], hl[:, q, c * P:(c + 1) * P], w, start=False, stop=(c == FC - 1))
                        ins.then_inc(y_ps, 1)

                expert_steps(pe, step)

            def attention_pe(b):
                m = 0
                for task in PLAN:
                    kind = task[0]
                    if kind in ("xT", "K", "V", "Q", "Y"):
                        if m:
                            pe.wait_ge(misc_free, b * NM + m)
                        else:
                            pe.wait_ge(xa_done, b * (QT + 1) + QT)
                    if kind == "xT":
                        for q in range(QT):
                            ins = t_.transpose(MB[:, q * P:(q + 1) * P], xa[:, q, :], ident[:])
                    elif kind == "K":
                        ins = three(MB[:], wks[:, 0, :], wks[:, 1, :], xTh[:], xTl[:])
                    elif kind == "V":
                        for q in range(QT):
                            c = slice(q * P, (q + 1) * P)
                            ins = three(MB[:, q * DH:(q + 1) * DH], xTh[:, c], xTl[:, c], wvs[:, 0, :], wvs[:, 1, :])
                    elif kind == "Q":
                        _, g, c = task
                        c = slice((2 * g + c) * P, (2 * g + c + 1) * P)
                        ins = three(MB[:], wqs[:, 0, c], wqs[:, 1, c], xTh[:], xTl[:])
                    elif kind == "Y":
                        g = task[1]
                        pe.wait_ge(ot_done, b * NU + QT * (g + 1))
                        for t in range(QT):
                            for c in range(2):
                                ins = t_.matmul(MB[:, t * D:(t + 1) * D], ot[:, g % 2, c, t * P:(t + 1) * P],
                                                wo_sb[:, 2 * g + c, :], start=(c == 0), stop=(c == 1))
                    if kind in ("xT", "K", "V", "Q", "Y"):
                        ins.then_inc(misc_ps, 1)
                        m += 1
                    elif kind == "S":
                        _, n, h = task
                        g, t = divmod(n, QT)
                        i = HG * n + h
                        w = max((t + 1) * P, 256)
                        if t == 0 and h == 0:
                            pe.wait_ge(misc_free, b * NM + MISC.index(("Q", g, 1)) + 1)
                        if i >= 3:
                            pe.wait_ge(s_done, b * NS + (i - 2))
                        q = qst[:, g % 2, h, t * P:(t + 1) * P]
                        t_.matmul(S_BANK[i % 3][:, 0:w], q, kst[:, 0, 0:w], start=True, stop=False)
                        t_.matmul(S_BANK[i % 3][:, 0:w], q, kst[:, 1, 0:w], start=False, stop=True).then_inc(s_ps, 1)
                    elif kind == "T":
                        _, n, jj = task
                        i = blk(n, jj)
                        if jj == 0:
                            pe.wait_ge(norm_done, b * NU + (n + 1))
                        if i >= 2:
                            pe.wait_ge(pl_done, b * NB + (i - 1))
                        for h in range(HG):
                            ins = t_.transpose(PT_BANK[i % 2][:, h * P:(h + 1) * P], prob[:, n % 2, h, jj * P:(jj + 1) * P], ident[:])
                        ins.then_inc(pt_ps, 1)
                    elif kind == "AV":
                        _, n, jj = task
                        i = blk(n, jj)
                        pe.wait_ge(pl_done, b * NB + (i + 1))
                        if jj == 0 and n >= 2:
                            pe.wait_ge(ot_done, b * NU + (n - 1))
                        t_.matmul(OT_BANK[n % 2][:], vst[:, jj, :], ph[:, i % 2, :], start=(jj == 0), stop=False)
                        t_.matmul(OT_BANK[n % 2][:], vst[:, jj, :], pl[:, i % 2, :], start=False, stop=(jj == n % QT)).then_inc(av_ps, 1)

            ffn_pe(0)
            if stop > 0:
                pe.wait_ge(split_lo, 6)
                pe.wait_ge(wa_in, 80)
                with pe.Fori(0, BATCH) as b:
                    attention_pe(b)
            if stop > 1:
                ffn_pe(1)


_INS = ["L0_attn_x", "L0_attn_Wq", "L0_attn_Wkv", "L0_attn_Wout", "L0_attn_bout", "L0_attn_rel_emb",
        "L0_ffn_gate_w", "L0_ffn_fc_w", "L0_ffn_proj_w"]


def kernel(**inputs):
    import concourse.bacc as bacc
    from concourse.bass_utils import run_bass_kernel_spmd

    nc = bacc.Bacc("TRN2", target_bir_lowering=False, num_devices=1)
    arrays, args = {}, []
    for name in _INS:
        a = np.ascontiguousarray(inputs[name])
        arrays[name] = a
        args.append(nc.dram_tensor(name, a.shape, mybir.dt.from_np(a.dtype), kind="ExternalInput").ap())
    args.append(nc.dram_tensor("out", (BATCH, SEQ, D), F32, kind="ExternalOutput").ap())
    build(nc, *args)
    r = run_bass_kernel_spmd(nc, [arrays], core_ids=[0])
    return r.results[0]["out"]
```

```python
from contextlib import ExitStack

import math

import numpy as np

import concourse.bass as bass
from concourse import mybir

P = 128
D = 128
BATCH, SEQ = 8, 512
TILES = BATCH * SEQ // P
E, TOPK, F = 8, 2, 512
FC = F // P
ETILES = TILES * TOPK + E
PAIRS = TILES * TOPK
H, DH = 16, 64
HG, NG = 4, 4
QT = SEQ // P
BUCKETS, MAX_DISTANCE = 32, 128
EPS = 1e-5
MASKED = -3.0e38

F32 = mybir.dt.float32
F32R = mybir.dt.float32r
BF16 = mybir.dt.bfloat16
I32 = mybir.dt.int32
ALU = mybir.AluOpType
ACT = mybir.ActivationFunctionType
AX = mybir.AxisListType.X
ds = bass.ds


def bucket(n):
    exact = BUCKETS // 2
    if n < exact:
        return n
    large = exact + int(math.log(n / exact) / math.log(MAX_DISTANCE / exact) * (BUCKETS - exact))
    return min(large, BUCKETS - 1)


def bucket_runs():
    runs = []
    for n in range(SEQ):
        if runs and runs[-1][0] == bucket(n):
            runs[-1][2] = n + 1
        else:
            runs.append([bucket(n), n, n + 1])
    return runs


def build(nc, x, Wq, Wkv, Wout, bout, rel_emb, gate_w, fc_w, proj_w, out, stop=99):
    ctx = ExitStack()
    with ctx:
        def sb(name, shape, dt=F32):
            return ctx.enter_context(nc.sbuf_tensor(name, shape, dt))

        def sem(name):
            return ctx.enter_context(nc.semaphore(name))

        xn_dram = [nc.dram_tensor(f"xn_dram{r}", [TILES * P, D], F32).ap() for r in range(2)]
        y2_dram = [nc.dram_tensor(f"y2_dram{r}", [TILES * P * TOPK, D], F32).ap() for r in range(2)]
        ROW = SEQ + P
        bias_dram = nc.dram_tensor("bias_dram", [H, P, ROW], F32).ap()

        x_sb = sb("x_sb", [P, TILES, D])
        ident = sb("ident", [P, P])
        ones_bf = sb("ones_bf", [P, P], BF16)
        before = sb("before", [P, P], BF16)
        iota_p = sb("iota_p", [P, P])
        pair_val = sb("pair_val", [P, TOPK])
        tile_val = sb("tile_val", [P, PAIRS])
        rev8 = sb("rev8", [P, E])
        tile_start = sb("tile_start", [P, ETILES])
        gate_sb = sb("gate_sb", [P, E])
        w1s = sb("w1s", [P, E, 2, F], F32R)
        w2s = sb("w2s", [P, E, FC, 2 * D], F32R)
        wqs = sb("wqs", [P, 2, H * DH], F32R)
        wks = sb("wks", [P, 2, P], F32R)
        wvs = sb("wvs", [P, 2, DH], F32R)
        wo_sb = sb("wo_sb", [P, H, D])
        bout_sb = sb("bout_sb", [P, D])
        bias_tab = sb("bias_tab", [P, H, SEQ])
        stats = sb("stats", [P, TILES, 6])
        lnt = sb("lnt", [P, 6, TILES])
        mean = sb("mean", [P, TILES])
        rstd = sb("rstd", [P, TILES])
        gw1 = sb("gw1", [P, TILES])
        gw2 = sb("gw2", [P, TILES])
        eps_t = sb("eps_t", [P, 1])
        base = nc.sbuf_base

        raw1 = bias_tab[:, 0:E, :]
        raw2 = bias_tab[:, E:2 * E, :].rearrange("p e (c d) -> p e c d", c=FC)

        ffn = ExitStack()
        with ffn:
            def fb(name, shape, dt=F32):
                return ffn.enter_context(nc.sbuf_tensor(name, shape, dt))

            xng = fb("xng", [P, 2, 4, D])
            xngT = fb("xngT", [P, 2, 4 * P])
            lg = fb("lg", [P, TILES, E])
            lg2 = fb("lg2", [P, TILES, E])
            eq = fb("eq", [P, TILES, E])
            oh = fb("oh", [P, TOPK, TILES, E])
            ohb = fb("ohb", [P, TILES, E], BF16)
            top = fb("top", [P, 4, TILES])
            scan = fb("scan", [P, 2, 16 + TILES, E])
            cnt = fb("cnt", [P, E])
            cnti = fb("cnti", [P, E], I32)
            padded = fb("padded", [P, E])
            escan = fb("escan", [P, 2, 4 + E])
            ends = fb("ends", [P, E])
            place = lg2
            pos = fb("pos", [P, PAIRS])
            posi = fb("posi", [P, 2, PAIRS], I32)
            posf = fb("posf", [P, 2, PAIRS])
            in_tile = fb("in_tile", [P, PAIRS, P], BF16)
            which = fb("which", [P, PAIRS, 2, ETILES], BF16)
            inv = fb("inv", [P, 2, ETILES])
            invt = fb("invt", [P, 2, ETILES])
            sidx = fb("sidx", [P, ETILES], I32)
            gidx = fb("gidx", [P, ETILES], I32)
            etf = fb("etf", [P, ETILES])
            etile = fb("etile", [P, ETILES], I32)
            wtmp = fb("wtmp", [P, 2, TILES])
            ecmp = in_tile[:, 0:ETILES // 2, :].bitcast(F32).rearrange("p a b -> p (a b)")[:, 0:ETILES * E].rearrange("p (t e) -> p t e", e=E)
            gring = fb("gring", [P, 4], I32)
            sring = fb("sring", [P, 4], I32)
            xr = fb("xr", [P, 4, D])
            xh = fb("xh", [P, 2, P], F32R)
            xl = fb("xl", [P, 2, P], F32R)
            hg = fb("hg", [P, 2, F])
            hh = fb("hh", [P, 2, F], F32R)
            hl = fb("hl", [P, 2, F], F32R)
            yt = fb("yt", [P, 2, D])
            yo = xng[:, 0, :, :]
            yc = in_tile[:, 0:PAIRS // 2, :].bitcast(F32).rearrange("p a b -> p (a b)").rearrange(
                "p (u q d) -> p u q d", u=2, q=4)
            rawq = which[:, 0:28, :, :].bitcast(F32).rearrange("p a b c -> p (a b c)")[:, 0:H * DH]
            rawkv = xr[:, 0, :]
            embT = fb("embT", [H, BUCKETS])
            brow = hg[0:H, :, :].rearrange("p a f -> p (a f)")[:, 0:SEQ + P]
        att = ExitStack()
        with att:
            def ab(name, shape, dt=F32):
                return att.enter_context(nc.sbuf_tensor(name, shape, dt))

            xa = ab("xa", [P, QT, D])
            xTh = ab("xTh", [P, SEQ], F32R)
            xTl = ab("xTl", [P, SEQ], F32R)
            kst = ab("kst", [P, 2, SEQ], F32R)
            vst = ab("vst", [P, QT, 2 * DH], F32R)
            qst = ab("qst", [P, 2, HG, SEQ], F32R)
            negs = ab("negs", [P, HG, SEQ])
            negmax = ab("negmax", [P, 8])
            prob = [ab(f"prob{t}", [P, HG, (t + 1) * P]) for t in range(QT)]
            lsum = ab("lsum", [P, 4, HG])
            rsum = ab("rsum", [P, 4, HG])
            ph = ab("ph", [P, 3, HG * P], F32R)
            pl = ab("pl", [P, 3, HG * P], F32R)
            ot = ab("ot", [P, 2, HG * P])

        bank = [ctx.enter_context(nc.psum_tensor(f"bank{i}", [P, 512], F32)) for i in range(8)]

        x_in = [sem(f"x_in{i}") for i in range(4)]
        w1_in, w2_in, wa_in, small_in = sem("w1_in"), sem("w2_in"), sem("wa_in"), sem("small_in")
        const_done, split_hi, split_lo = sem("const_done"), sem("split_hi"), sem("split_lo")
        brow_done, brow_out, bias_in = sem("brow_done"), sem("brow_out"), sem("bias_in")
        dstep = sem("dstep")
        vstep = [0]
        ln_ln = sem("ln_ln")
        ln_var = sem("ln_var")
        ln_done = sem("ln_done")
        xn_done, xnT_ps, xnT_sb, logit_ps = (sem(n) for n in ("xn_done", "xnT_ps", "xnT_sb", "logit_ps"))
        xn_out = [sem(f"xn_out{i}") for i in range(2)]
        gathered = [sem(f"gathered{i}") for i in range(4)]
        scattered = [sem(f"scattered{i}") for i in range(4)]
        lg_diff, lg_exp, hot_done, prefix_ps, onehot_done, inv_ps, route_done = (
            sem(n) for n in ("lg_diff", "lg_exp", "hot_done", "prefix_ps", "onehot_done", "inv_ps", "route_done"))
        gring_done, xrT_ps, xh_done, xl_done, up_ps, gelu_done, hT_ps, hh_done, hl_done, y_ps, yt_done, yo_done = (
            sem(n) for n in ("gring_done", "xrT_ps", "xh_done", "xl_done", "up_ps", "gelu_done", "hT_ps",
                             "hh_done", "hl_done", "y_ps", "yt_done", "yo_done"))
        y2_in = [sem("y2_in0"), sem("y2_in1")]
        comb1, combined, out_done = sem("comb1"), sem("combined"), sem("out_done")
        xa_done, misc_ps, misc_hi, misc_free, s_ps, s_done, exp_done, rsum_done, norm_done = (
            sem(n) for n in ("xa_done", "misc_ps", "misc_hi", "misc_free", "s_ps", "s_done", "exp_done",
                             "rsum_done", "norm_done"))
        pt_ps, ph_done, pl_done, av_ps, bout_done, ot_done = (
            sem(n) for n in ("pt_ps", "ph_done", "pl_done", "av_ps", "bout_done", "ot_done"))

        block = ctx.enter_context(nc.Block())

        LAST = ETILES + 6
        MAIN0 = 8
        assert (ETILES - MAIN0) % 4 == 0

        def expert_steps(eng, step):
            for k in range(MAIN0):
                step(k, k, 0)
            with eng.Fori(0, (ETILES - MAIN0) // 4) as i:
                for u in range(4):
                    step(i * 4 + (MAIN0 + u), MAIN0 + u, i, loop=True)
            for k in range(ETILES, LAST):
                step(k, k, 0)

        carriers = {}

        def apart(eng):
            eng.reg_alu(carriers[eng], carriers[eng], 1, op=ALU.bitwise_and)

        def carrier(eng):
            carriers[eng] = eng.alloc_register("carrier")
            eng.reg_mov(carriers[eng], 1)

        def carried(eng):
            eng.wait_ge(const_done, carriers[eng])

        def dmas(r, i, s):
            return (i + (r * ETILES // 4 + s // 4 + 1)) * 16

        def on(k, lag, loop):
            return loop or 0 <= k - lag < ETILES

        def attention_plan():
            units = NG * QT
            blocks = [(n, jj) for n in range(units) for jj in range(n % QT + 1)]
            before_unit = {1: [("Q", 0, 1, 0), ("Q", 0, 1, 1)], 5: [("Q", 0, 2, 0), ("Q", 0, 2, 1)],
                           9: [("Q", 0, 3, 0), ("Q", 0, 3, 1)]}
            before_unit |= {10: [("LN", 1)], 12: [("xT", 1)], 13: [("Q", 1, 0, 0), ("Q", 1, 0, 1)], 14: [("K", 1)]}
            main, seen, late = [("V", 0)], 0, []
            scored, lead = [], []

            def tick():
                for item in [x for x in late if x[0] <= 0]:
                    late.remove(item)
                    main.append(item[1])
                for x in late:
                    x[0] -= 1

            for n in range(units):
                main.extend(before_unit.get(n, []))
                first = [("T", n, jj) for jj in range(n % QT + 1)]
                nxt = n + 2
                second = [("S", nxt // units, nxt % units, h) for h in range(HG)]
                a, b = len(first), len(second)
                mix = sorted([((i + 0.5) / a, 0, x) for i, x in enumerate(first)]
                             + [((i + 0.5) / b, 1, x) for i, x in enumerate(second)])
                for _, _, x in mix:
                    main.append(x)
                    if x[0] == "S":
                        scored.append(x)
                        if len(scored) >= 2:
                            main.append(("E",) + scored[-2][1:])
                        if x[3] == 1 and len(scored) >= 4:
                            main.append(("R",) + scored[-3][1:3])
                    else:
                        if seen >= 1:
                            main.append(("L",) + blocks[seen - 1])
                        if seen >= 2:
                            pn, pj = blocks[seen - 2]
                            main.append(("AV", pn, pj))
                            if pj == pn % QT:
                                main.append(("O", pn))
                                late.append([1, ("Y", pn)])
                        seen += 1
                    tick()
            main.append(("L",) + blocks[-1])
            main.append(("E",) + scored[-1][1:])
            main.append(("AV",) + blocks[-2])
            main.append(("AV",) + blocks[-1])
            main.append(("O", units - 1))
            main.append(("R",) + scored[-1][1:3])
            main += [x for _, x in late]
            main.append(("Y", units - 1))
            return main

        def prologue_plan():
            plan = [("LN", 0), ("xT", 0), ("K", 0), ("Q", 0, 0, 0), ("Q", 0, 0, 1)]
            for n in range(2):
                plan += [("S", 0, n, h) for h in range(HG)] + [("E", 0, n, h) for h in range(HG)] + [("R", 0, n)]
            return plan

        FIRST, PLAN = prologue_plan(), attention_plan()
        FINAL = [x for x in PLAN if not (x[0] in ("LN", "xT", "K", "Q", "S", "E", "R") and x[1] == 1)]
        USERS = ("xT", "K", "V", "Q", "Y")
        HIGHS = {"xT": 1, "K": 1, "V": 1, "Q": 2, "Y": 0}

        def tally(plan):
            m = hi = 0
            out = []
            for x in plan:
                out.append((m, hi))
                if x[0] in USERS:
                    m, hi = m + 1, hi + HIGHS[x[0]]
            return out, m, hi

        TALLY, NM, NHI = tally(PLAN)
        _, PRE, PREHI = tally(FIRST)
        NS = NG * QT * HG
        NU = NG * QT
        NB = NG * QT * (QT + 1) // 2
        MISC_END = PRE + (BATCH - 1) * NM + tally(FINAL)[1]

        def walk(plan, b):
            counts, _, _ = tally(plan)
            for x, (m, hi) in zip(plan, counts):
                yield x, (m if plan is FIRST else b * NM + (PRE + m)), (hi if plan is FIRST else b * NHI + (PREHI + hi))

        def place_of(plan, b, task):
            m = tally(plan)[0][plan.index(task)][0] + 1
            return m if plan is FIRST else b * NM + (PRE + m)

        def attention(eng, run):
            run(FIRST, 0)
            with eng.Fori(0, BATCH - 1) as b:
                run(PLAN, b)
            run(FINAL, BATCH - 1)

        def blk(n, jj):
            g, t = divmod(n, QT)
            return g * (QT * (QT + 1) // 2) + t * (t + 1) // 2 + jj

        S_BANK = [bank[0], bank[1]]
        PT_BANK = [bank[2], bank[3], bank[4]]
        OT_BANK = [bank[5], bank[6]]
        MB = bank[7]

        @block.sync
        def _(sp):
            xt = x.rearrange("b (t p) d -> p (b t) d", p=P)
            sp.dma_start(x_sb[:, 0:8, :], xt[:, 0:8, :]).then_inc(x_in[0], 16)
            sp.dma_start(gate_sb[:], gate_w).then_inc(small_in, 16)
            for i in range(1, 4):
                sp.dma_start(x_sb[:, 8 * i:8 * i + 8, :], xt[:, 8 * i:8 * i + 8, :]).then_inc(x_in[i], 16)
            sp.dma_start(raw1, fc_w.rearrange("e d f -> d e f")).then_inc(w1_in, 16)
            sp.dma_start(raw2, proj_w.rearrange("e (c p) d -> p e c d", p=P)).then_inc(w2_in, 16)
            sp.wait_ge(brow_done, 1)
            sp.dma_start(bias_dram, brow.unsqueeze(1).to_broadcast([H, P, ROW])).then_inc(brow_out, 16)
            sp.wait_ge(brow_out, 16)
            sp.wait_ge(split_lo, 2)
            src = bass.AP(tensor=bias_dram.tensor, offset=bias_dram.offset + P - 1,
                          ap=[[ROW - 1, P], [P * ROW, H], [1, SEQ]])
            sp.dma_start(bias_tab[:], src).then_inc(bias_in, 16)

            def ffn_sp(r):
                xd = xn_dram[r].rearrange("(t p) d -> p t d", p=P)
                with sp.Fori(0, TILES // 8) as i:
                    for u in range(2):
                        gi = i * 2 + u
                        sp.wait_ge(xn_done, r * TILES + gi * 4 + 4)
                        sp.dma_start(xd[:, ds(gi * 4, 4), :], xng[:, u, :, :]).then_inc(xn_out[u], 16)
                for s in range(4):
                    sp.wait_ge(scattered[s], 4 * ETILES * (r + 1))
                yd = y2_dram[r].rearrange("(t p k) d -> p t (k d)", p=P, k=TOPK)
                for gi in range(2):
                    sp.dma_start(yc[:, gi, :, :], yd[:, 4 * gi:4 * gi + 4, :]).then_inc(y2_in[gi], 16)
                with sp.Fori(1, TILES // 8) as i:
                    for u in range(2):
                        gi = i * 2 + u
                        sp.wait_ge(combined, r * TILES + gi * 4 - 4)
                        sp.dma_start(yc[:, u, :, :], yd[:, ds(gi * 4, 4), :]).then_inc(y2_in[u], 16)

            ffn_sp(0)
            if stop > 1:
                ffn_sp(1)
            ot_ = out.rearrange("b (t p) d -> p (b t) d", p=P)
            sp.wait_ge(combined if stop != 1 else misc_free, (2 if stop > 1 else 1) * TILES if stop != 1 else MISC_END)
            sp.dma_start(ot_, x_sb[:]).then_inc(out_done, 16)
            sp.wait_ge(out_done, 16)

        @block.gpsimd
        def _(gp):
            g = nc.gpsimd
            carrier(gp)
            g.memset(ident[:], 0.0).then_inc(const_done, 1)
            g.memset(before[:], 1.0).then_inc(const_done, 1)
            g.memset(ones_bf[:], 1.0).then_inc(const_done, 1)
            gp.wait_ge(const_done, 3)
            g.affine_select(out=ident[:], in_=ident[:], compare_op=ALU.not_equal, fill=1.0,
                            base=0, pattern=[[-1, P]], channel_multiplier=1).then_inc(const_done, 1)
            g.affine_select(out=before[:], in_=before[:], compare_op=ALU.is_gt, fill=0.0,
                            base=0, pattern=[[1, P]], channel_multiplier=-1).then_inc(const_done, 1)
            iota = dict(allow_small_or_imprecise_dtypes=True)
            g.iota(iota_p[:], pattern=[[1, P]], base=0, channel_multiplier=0, **iota).then_inc(const_done, 1)
            g.iota(pair_val[:], pattern=[[1, TOPK]], base=1, channel_multiplier=2, **iota).then_inc(const_done, 1)
            g.iota(tile_val[:], pattern=[[0, TOPK], [1, TILES]], base=0, channel_multiplier=0, **iota).then_inc(const_done, 1)
            g.iota(rev8[:], pattern=[[-1, E]], base=E, channel_multiplier=0, **iota).then_inc(const_done, 1)
            g.iota(tile_start[:], pattern=[[P, ETILES]], base=0, channel_multiplier=0, **iota).then_inc(const_done, 1)
            g.memset(eps_t[:], EPS).then_inc(const_done, 1)
            g.memset(scan[:, :, 0:17, :], 0.0).then_inc(const_done, 1)
            g.memset(escan[:, :, 0:5], 0.0).then_inc(const_done, 1)
            g.dma_start(rawq, Wq).then_inc(wa_in, 16)
            g.dma_start(rawkv, Wkv).then_inc(wa_in, 16)
            for z in range(2):
                g.dma_start(wo_sb[z * DH:(z + 1) * DH, :, :], Wout.rearrange("(h p) d -> p h d", p=DH)).then_inc(wa_in, 16)
            g.dma_start(embT[:], rel_emb.rearrange("k h -> h k"), allow_slow_non_contiguous=True).then_inc(wa_in, 16)
            g.dma_start(bout_sb[:], bout.rearrange("(a d) -> a d", a=1).to_broadcast([P, D])).then_inc(wa_in, 16)

            def ffn_pool(r):
                k0 = r * ETILES
                if r:
                    gp.wait_ge(misc_free, MISC_END)
                    g.memset(scan[:, :, 0:17, :], 0.0).then_inc(const_done, 1)
                    g.memset(escan[:, :, 0:5], 0.0).then_inc(const_done, 1)
                gp.wait_ge(route_done, r + 1)
                for u in range(2):
                    gp.wait_ge(xn_out[u], 16 * (TILES // 8) * (r + 1))

                def step(k, s, i, loop=False):
                    if on(k, 0, loop):
                        gp.wait_ge(gring_done, k0 + k + 1)
                        if loop or k >= 4:
                            gp.wait_ge(xrT_ps, k0 + k - 3)
                        apart(gp)
                        g.indirect_dma_start(out=xr[:, s % 4, :], out_offset=None, in_=xn_dram[r],
                                             in_offset=bass.IndirectOffsetOnAxis(ap=gring[:, s % 4:s % 4 + 1], axis=0),
                                             ).then_inc(gathered[s % 4], 16)
                    if on(k, 6, loop):
                        gp.wait_ge(yo_done, k0 + k - 5)
                        q = (s - 6) % 4
                        apart(gp)
                        g.indirect_dma_start(out=y2_dram[r], in_=yo[:, q, :], in_offset=None,
                                             out_offset=bass.IndirectOffsetOnAxis(ap=sring[:, q:q + 1], axis=0),
                                             bounds_check=TILES * P * TOPK - 1, oob_is_err=False).then_inc(scattered[q], 16)

                expert_steps(gp, step)

            ffn_pool(0)
            if stop > 0:
                def run(plan, b):
                    for task, _, _ in walk(plan, b):
                        if task[0] == "LN":
                            gp.wait_ge(xa_done, (b + (task[1] + 1)) * QT)
                            xb = x_sb[:, ds((b + task[1]) * QT, QT), :]
                            g.tensor_tensor(out=xb, in0=xb, in1=bout_sb[:].unsqueeze(1).to_broadcast([P, QT, D]),
                                            op=ALU.add).then_inc(bout_done, 1)
                        elif task[0] == "R":
                            _, nb, n = task
                            gp.wait_ge(rsum_done, (b + nb) * NU + (n + 1))
                            pv = prob[n % QT][:]
                            g.tensor_tensor(out=pv, in0=pv, in1=rsum[:, n % 4, :].unsqueeze(2).to_broadcast([P, HG, (n % QT + 1) * P]),
                                            op=ALU.mult).then_inc(norm_done, 1)

                attention(gp, run)
            if stop > 1:
                ffn_pool(1)
            carried(gp)

        @block.scalar
        def _(act):
            a = nc.scalar
            act.wait_ge(w1_in, 16)
            a.activation(w1s[:, :, 0, :], raw1, ACT.Copy).then_inc(split_hi, 1)
            act.wait_ge(w2_in, 16)
            a.activation(w2s[:, :, :, 0:D], raw2, ACT.Copy).then_inc(split_hi, 1)
            act.wait_ge(wa_in, 96)
            a.activation(wqs[:, 0, :], rawq, ACT.Copy).then_inc(split_hi, 1)
            a.activation(wks[:, 0, 0:DH], rawkv[:, 0:DH], ACT.Copy).then_inc(split_hi, 1)
            a.activation(wks[:, 0, DH:P], rawkv[:, 0:DH], ACT.Copy).then_inc(split_hi, 1)
            a.activation(wvs[:, 0, :], rawkv[:, DH:P], ACT.Copy).then_inc(split_hi, 1)

            def ln_act(r):
                act.wait_ge(const_done, 13)
                act.wait_ge(ln_var, r + 1)
                a.activation(lnt[:, 3, :], lnt[:, 2, :], ACT.Ln, bias=eps_t[:, 0:1]).then_inc(ln_ln, 1)
                act.wait_ge(ln_ln, 2 * r + 1)
                a.activation(lnt[:, 4, :], lnt[:, 3, :], ACT.Exp, scale=-0.5).then_inc(ln_ln, 1)

            def ffn_act(r):
                ln_act(2 * r)
                with act.Fori(0, TILES // 8) as i:
                    for u in range(2):
                        act.wait_ge(xnT_ps, r * (TILES // 4) + i * 2 + (u + 1))
                        a.activation(xngT[:, u, :], bank[u][:], ACT.Copy).then_inc(xnT_sb, 1)
                act.wait_ge(lg_diff, r + 1)
                a.activation(wtmp[:, 1, :], wtmp[:, 0, :], ACT.Exp).then_inc(lg_exp, 1)
                k0 = r * ETILES

                def step(k, s, i, loop=False):
                    if on(k, 2, loop):
                        q = (s - 2) % 2
                        act.wait_ge(xrT_ps, k0 + k - 1)
                        if loop or k >= 4:
                            act.wait_ge(up_ps, k0 + k - 3)
                        a.activation(xh[:, q, :], bank[q][:, 0:P], ACT.Copy).then_inc(xh_done, 1)
                    if on(k, 3, loop):
                        q = (s - 3) % 2
                        act.wait_ge(up_ps, k0 + k - 2)
                        if loop or k >= 5:
                            act.wait_ge(hT_ps, k0 + k - 4)
                        a.activation(hg[:, q, :], bank[2 + q][:], ACT.Gelu).then_inc(gelu_done, 1)
                    if on(k, 4, loop):
                        q = (s - 4) % 2
                        act.wait_ge(hT_ps, k0 + k - 3)
                        if loop or k >= 6:
                            act.wait_ge(y_ps, k0 + k - 5)
                        a.activation(hh[:, q, :], bank[4 + q][:], ACT.Copy).then_inc(hh_done, 1)
                    if on(k, 5, loop):
                        q = (s - 5) % 2
                        act.wait_ge(y_ps, k0 + k - 4)
                        if loop or k >= 7:
                            act.wait_ge(yo_done, k0 + k - 6)
                        a.activation(yt[:, q, :], bank[6 + q][:, D:2 * D], ACT.Copy).then_inc(yt_done, 1)

                expert_steps(act, step)

            def attention_act(plan, b):
                for task, m, hi in walk(plan, b):
                    kind = task[0]
                    if kind in ("xT", "K", "V"):
                        act.wait_ge(misc_ps, m + 1)
                        dst = {"xT": xTh[:], "K": kst[:, 0, :], "V": vst[:, :, 0:DH]}[kind]
                        src = MB[:, 0:QT * DH].rearrange("p (t d) -> p t d", d=DH) if kind == "V" else MB[:]
                        a.activation(dst, src, ACT.Copy).then_inc(misc_hi, 1)
                    elif kind == "Q":
                        _, _, g, c = task
                        act.wait_ge(misc_ps, m + 1)
                        for o in range(2):
                            a.activation(qst[0:DH, g % 2, 2 * c + o, :], MB[DH * o:DH * o + DH, :], ACT.Copy,
                                         scale=DH ** -0.5).then_inc(misc_hi, 1)
                    elif kind == "E":
                        _, nb, n, h = task
                        w = (n % QT + 1) * P
                        act.wait_ge(s_done, (b + nb) * NS + (HG * n + h + 1))
                        a.activation(prob[n % QT][:, h, :], negs[:, h, 0:w], ACT.Exp, scale=-1.0,
                                     bias=negmax[:, (HG * n + h) % 8:(HG * n + h) % 8 + 1],
                                     accum_out=lsum[:, n % 4, h:h + 1]).then_inc(exp_done, 1)
                    elif kind == "T":
                        _, n, jj = task
                        i = blk(n, jj)
                        act.wait_ge(pt_ps, b * NB + (i + 1))
                        if i >= 3:
                            act.wait_ge(av_ps, b * NB + (i - 2))
                        a.activation(ph[:, i % 3, :], PT_BANK[i % 3][:], ACT.Copy).then_inc(ph_done, 1)
                    elif kind == "O":
                        n = task[1]
                        act.wait_ge(av_ps, b * NB + (blk(n, n % QT) + 1))
                        if n >= 2:
                            act.wait_ge(misc_ps, place_of(plan, b, ("Y", n - 2)))
                        a.activation(ot[:, n % 2, :], OT_BANK[n % 2][:], ACT.Copy).then_inc(ot_done, 1)

            ffn_act(0)
            if stop > 0:
                ln_act(1)
                attention(act, attention_act)
            if stop > 1:
                ffn_act(1)

        @block.vector
        def _(dve):
            v = nc.vector
            carrier(dve)

            def step_done(ins):
                vstep[0] += 1
                ins.then_inc(dstep, 1)
                dve.wait_ge(dstep, vstep[0])

            def async_done(ins):
                vstep[0] += 1
                ins.then_inc(dstep, 1)

            def waited():
                dve.wait_ge(dstep, vstep[0])

            def layer_norm_stats(r, first=False):
                if first:
                    for c in range(4):
                        dve.wait_ge(x_in[c], 16)
                with dve.Fori(0, TILES) as i:
                    v.bn_stats(out=stats[:, ds(i, 1), :].rearrange("p a s -> p (a s)"),
                               in_=x_sb[:, ds(i, 1), :].rearrange("p a d -> p (a d)")).then_inc(dstep, 1)
                vstep[0] += TILES
                waited()
                me, m2e, mo, m2o = (stats[:, :, s] for s in (1, 2, 4, 5))
                async_done(v.tensor_tensor(lnt[:, 0, :], me, mo, ALU.add))
                async_done(v.tensor_tensor(lnt[:, 1, :], me, mo, ALU.subtract))
                async_done(v.tensor_tensor(lnt[:, 5, :], m2e, m2o, ALU.add))
                waited()
                async_done(v.tensor_scalar(mean[:], lnt[:, 0, :], 0.5, None, ALU.mult))
                step_done(v.scalar_tensor_tensor(out=lnt[:, 3, :], in0=lnt[:, 1, :], scalar=D / 4.0, in1=lnt[:, 1, :],
                                                 op0=ALU.mult, op1=ALU.mult))
                step_done(v.tensor_tensor(lnt[:, 5, :], lnt[:, 5, :], lnt[:, 3, :], ALU.add))
                v.tensor_scalar(lnt[:, 2, :], lnt[:, 5, :], 1.0 / D, None, ALU.mult).then_inc(ln_var, 1)
                dve.wait_ge(ln_ln, 2 * r + 2)
                y = lnt[:, 4, :]
                step_done(v.tensor_tensor(lnt[:, 0, :], y, y, ALU.mult))
                step_done(v.scalar_tensor_tensor(out=lnt[:, 1, :], in0=lnt[:, 2, :], scalar=EPS, in1=lnt[:, 0, :],
                                                 op0=ALU.add, op1=ALU.mult))
                step_done(v.tensor_scalar(lnt[:, 0, :], lnt[:, 1, :], -0.5, 1.5, ALU.mult, ALU.add))
                step_done(v.tensor_tensor(rstd[:], y, lnt[:, 0, :], ALU.mult))

            def routing(r):
                bc = lambda t: t.unsqueeze(2).to_broadcast([P, TILES, E])
                dve.wait_ge(logit_ps, (r + 1) * TILES)
                if r:
                    carried(dve)
                step_done(v.tensor_copy(lg[:].rearrange("p t e -> p (t e)"), bank[2][:, 0:TILES * E]))
                rev = rev8[:].unsqueeze(1).to_broadcast([P, TILES, E])
                src = lg
                for c in range(TOPK):
                    step_done(v.tensor_reduce(out=top[:, c, :], in_=src[:], op=ALU.max, axis=AX))
                    step_done(v.tensor_tensor(eq[:], src[:], bc(top[:, c, :]), ALU.is_equal))
                    step_done(v.tensor_tensor(eq[:], eq[:], rev, ALU.mult))
                    step_done(v.tensor_reduce(out=top[:, 2 + c, :], in_=eq[:], op=ALU.max, axis=AX))
                    step_done(v.tensor_tensor(oh[:, c, :, :], rev, bc(top[:, 2 + c, :]), ALU.is_equal))
                    if c == 0:
                        step_done(v.scalar_tensor_tensor(out=lg2[:], in0=oh[:, 0, :, :], scalar=MASKED, in1=lg[:],
                                                         op0=ALU.mult, op1=ALU.add))
                        src = lg2
                v.tensor_tensor(ohb[:], oh[:, 0, :, :], oh[:, 1, :, :], ALU.add).then_inc(hot_done, 1)
                v.tensor_tensor(wtmp[:, 0, :], top[:, 1, :], top[:, 0, :], ALU.subtract).then_inc(lg_diff, 1)
                dve.wait_ge(prefix_ps, r + 1)
                if r:
                    dve.wait_ge(const_done, 15)
                tot = bank[3][:, 0:TILES * E].rearrange("p (t e) -> p t e", e=E)
                step_done(v.tensor_copy(scan[:, 0, 17:16 + TILES, :], tot[:, 0:TILES - 1, :]))
                cur = 0
                for sh in (1, 2, 4, 8, 16):
                    step_done(v.tensor_tensor(scan[:, 1 - cur, 16:, :], scan[:, cur, 16:, :],
                                              scan[:, cur, 16 - sh:16 + TILES - sh, :], ALU.add))
                    cur = 1 - cur
                step_done(v.tensor_tensor(cnt[:], scan[:, cur, 15 + TILES, :], tot[:, TILES - 1, :], ALU.add))
                step_done(v.tensor_scalar(cnti[:], cnt[:], float(P - 1), None, ALU.add))
                step_done(v.tensor_scalar(cnti[:], cnti[:], 7, 7, ALU.logical_shift_right, ALU.logical_shift_left))
                async_done(v.tensor_copy(padded[:], cnti[:]))
                step_done(v.tensor_copy(escan[:, 0, 5:4 + E], cnti[:, 0:E - 1]))
                ec = 0
                for sh in (1, 2, 4):
                    step_done(v.tensor_tensor(escan[:, 1 - ec, 4:], escan[:, ec, 4:], escan[:, ec, 4 - sh:4 + E - sh], ALU.add))
                    ec = 1 - ec
                ebase = escan[:, ec, 4:]
                async_done(v.tensor_tensor(ends[:], ebase, padded[:], ALU.add))
                step_done(v.tensor_tensor(place[:], scan[:, cur, 16:, :], ebase.unsqueeze(1).to_broadcast([P, TILES, E]), ALU.add))
                step_done(v.tensor_tensor(place[:], place[:], bank[4][:, 0:TILES * E].rearrange("p (t e) -> p t e", e=E), ALU.add))
                for c in range(TOPK):
                    step_done(v.tensor_tensor(eq[:], place[:], oh[:, c, :, :], ALU.mult))
                    step_done(v.tensor_reduce(out=pos[:, c * TILES:(c + 1) * TILES], in_=eq[:], op=ALU.add, axis=AX))
                step_done(v.tensor_copy(posi[:, 0, :], pos[:]))
                async_done(v.tensor_scalar(posi[:, 1, :], posi[:, 0, :], 7, None, ALU.logical_shift_right))
                waited()
                step_done(v.tensor_scalar(posi[:, 0, :], posi[:, 0, :], P - 1, None, ALU.bitwise_and))
                step_done(v.tensor_copy(posf[:], posi[:]))
                step_done(v.tensor_tensor(ecmp, tile_start[:].unsqueeze(2).to_broadcast([P, ETILES, E]),
                                          ends[:].unsqueeze(1).to_broadcast([P, ETILES, E]), ALU.is_ge))
                step_done(v.tensor_reduce(out=etf[:], in_=ecmp[:, :, 0:E - 1], op=ALU.add, axis=AX))
                async_done(v.tensor_copy(etile[:], etf[:]))
                async_done(v.tensor_tensor(in_tile[:], iota_p[:].unsqueeze(1).to_broadcast([P, PAIRS, P]),
                                           posf[:, 0, :].unsqueeze(2).to_broadcast([P, PAIRS, P]), ALU.is_equal))
                step_done(v.tensor_tensor(posf[:, 1, :], pos[:], posf[:, 0, :], ALU.subtract))
                ts = tile_start[:].unsqueeze(1).to_broadcast([P, PAIRS, ETILES])
                step_done(v.tensor_tensor(which[:, :, 0, :], ts, posf[:, 1, :].unsqueeze(2).to_broadcast([P, PAIRS, ETILES]), ALU.is_equal))
                async_done(v.tensor_tensor(which[:, :, 1, :], which[:, :, 0, :],
                                           tile_val[:].unsqueeze(2).to_broadcast([P, PAIRS, ETILES]), ALU.mult))
                waited()
                for c in range(TOPK):
                    last = v.tensor_scalar(which[:, c * TILES:(c + 1) * TILES, 0, :], which[:, c * TILES:(c + 1) * TILES, 0, :],
                                           pair_val[:, c:c + 1], None, ALU.mult)
                    if c < TOPK - 1:
                        async_done(last)
                last.then_inc(onehot_done, 1)
                dve.wait_ge(lg_exp, r + 1)
                step_done(v.tensor_scalar(wtmp[:, 0, :], wtmp[:, 1, :], 2.0, 2.0, ALU.mult, ALU.add))
                step_done(v.reciprocal(gw1[:], wtmp[:, 0, :]))
                step_done(v.tensor_tensor(gw2[:], gw1[:], wtmp[:, 1, :], ALU.mult))
                dve.wait_ge(inv_ps, r + 1)
                step_done(v.tensor_copy(inv[:].rearrange("p a b -> p (a b)"), bank[5][:, 0:2 * ETILES]))
                step_done(v.scalar_tensor_tensor(out=invt[:, 0, :], in0=inv[:, 1, :], scalar=2.0 * P, in1=inv[:, 0, :],
                                                 op0=ALU.mult, op1=ALU.add))
                step_done(v.tensor_scalar(invt[:, 1, :], invt[:, 0, :], 0.0, 1.0e5, ALU.is_equal, ALU.mult))
                step_done(v.scalar_tensor_tensor(out=inv[:, 0, :], in0=invt[:, 0, :], scalar=-1.0, in1=invt[:, 1, :],
                                                 op0=ALU.add, op1=ALU.add))
                step_done(v.tensor_copy(sidx[:], inv[:, 0, :]))
                step_done(v.tensor_scalar(invt[:, 1, :], invt[:, 0, :], -1.0, 0.0, ALU.add, ALU.max))
                step_done(v.tensor_copy(gidx[:], invt[:, 1, :]))
                v.tensor_scalar(gidx[:], gidx[:], 1, None, ALU.logical_shift_right).then_inc(route_done, 1)
                dve.wait_ge(route_done, r + 1)

            def ffn_dve(r):
                layer_norm_stats(2 * r, first=(r == 0))
                if r == 0:
                    dve.wait_ge(const_done, 13)
                g0 = r * (TILES // 4)

                def norm_group(gi, u):
                    for q in range(4):
                        t = gi * 4 + q
                        v.tensor_scalar(xng[:, u, q, :], x_sb[:, ds(t, 1), :].rearrange("p a d -> p (a d)"),
                                        mean[:, ds(t, 1)], rstd[:, ds(t, 1)], ALU.subtract, ALU.mult).then_inc(xn_done, 1)

                for u in range(2):
                    norm_group(u, u)
                with dve.Fori(1, TILES // 8) as i:
                    for u in range(2):
                        gi = i * 2 + u
                        dve.wait_ge(xnT_ps, g0 + gi - 1)
                        dve.wait_ge(xn_out[u], (i + r * (TILES // 8)) * 16)
                        norm_group(gi, u)
                routing(r)
                k0 = r * ETILES

                def step(k, s, i, loop=False):
                    if on(k, 0, loop):
                        if loop or k >= 4:
                            dve.wait_ge(gathered[s % 4], dmas(r, i, s - 4))
                        v.tensor_copy(gring[:, s % 4:s % 4 + 1], gidx[:, ds(k, 1)]).then_inc(gring_done, 1)
                    if on(k, 2, loop):
                        q = (s - 2) % 2
                        dve.wait_ge(xh_done, k0 + k - 1)
                        v.tensor_tensor(xl[:, q, :], bank[q][:, 0:P], xh[:, q, :].bitcast(F32), ALU.subtract).then_inc(xl_done, 1)
                    if on(k, 4, loop):
                        q = (s - 4) % 2
                        dve.wait_ge(hh_done, k0 + k - 3)
                        v.tensor_tensor(hl[:, q, :], bank[4 + q][:], hh[:, q, :].bitcast(F32), ALU.subtract).then_inc(hl_done, 1)
                    if on(k, 5, loop):
                        q = (s - 5) % 2
                        dve.wait_ge(yt_done, k0 + k - 4)
                        if loop or k >= 9:
                            dve.wait_ge(scattered[(s - 5) % 4], dmas(r, i, s - 9))
                        v.tensor_copy(sring[:, (s - 5) % 4:(s - 5) % 4 + 1], sidx[:, ds(k - 5, 1)])
                        v.tensor_tensor(yo[:, (s - 5) % 4, :], bank[6 + q][:, 0:D], yt[:, q, :], ALU.add).then_inc(yo_done, 1)

                expert_steps(dve, step)
                for gi in range(2):
                    combine(r, gi, gi, 1)
                with dve.Fori(1, TILES // 8) as i:
                    for u in range(2):
                        combine(r, i * 2 + u, u, i + 1)

            def combine(r, gi, u, nth):
                dve.wait_ge(y2_in[u], (r * (TILES // 8) + nth) * 16)
                for c, w in ((0, gw1), (1, gw2)):
                    for q in range(4):
                        t = gi * 4 + q
                        xt = x_sb[:, ds(t, 1), :].rearrange("p a d -> p (a d)")
                        ins = v.scalar_tensor_tensor(out=xt, in0=yc[:, u, q, c * D:(c + 1) * D], scalar=w[:, ds(t, 1)],
                                                     in1=xt, op0=ALU.mult, op1=ALU.add)
                        ins.then_inc(comb1 if c == 0 else combined, 1)
                    if c == 0:
                        dve.wait_ge(comb1, r * TILES + gi * 4 + 4)

            def attention_dve(plan, b):
                for task, m, hi in walk(plan, b):
                    kind = task[0]
                    if kind == "LN":
                        for q in range(QT):
                            t = (b + task[1]) * QT + q
                            v.tensor_scalar(xa[:, q, :], x_sb[:, ds(t, 1), :].rearrange("p a d -> p (a d)"),
                                            mean[:, ds(t, 1)], rstd[:, ds(t, 1)], ALU.subtract, ALU.mult).then_inc(xa_done, 1)
                    elif kind in ("xT", "K", "V"):
                        dve.wait_ge(misc_hi, hi + 1)
                        hi_t, dst = {"xT": (xTh[:], xTl[:]), "K": (kst[:, 0, :], kst[:, 1, :]),
                                     "V": (vst[:, :, 0:DH], vst[:, :, DH:])}[kind]
                        src = MB[:, 0:QT * DH].rearrange("p (t d) -> p t d", d=DH) if kind == "V" else MB[:]
                        v.tensor_tensor(dst, src, hi_t.bitcast(F32), ALU.subtract).then_inc(misc_free, 1)
                    elif kind == "Q":
                        _, _, g, c = task
                        for o in range(2):
                            dve.wait_ge(misc_hi, hi + (o + 1))
                            ins = v.scalar_tensor_tensor(out=qst[DH:P, g % 2, 2 * c + o, :], in0=MB[DH * o:DH * o + DH, :],
                                                         scalar=DH ** -0.5, in1=qst[0:DH, g % 2, 2 * c + o, :].bitcast(F32),
                                                         op0=ALU.mult, op1=ALU.subtract)
                        ins.then_inc(misc_free, 1)
                    elif kind == "Y":
                        n = task[1]
                        dve.wait_ge(misc_ps, m + 1)
                        if n < QT:
                            dve.wait_ge(bout_done, b + 1)
                        else:
                            dve.wait_ge(misc_free, place_of(plan, b, ("Y", n - QT)))
                        xt = x_sb[:, ds(b * QT + n % QT, 1), :].rearrange("p a d -> p (a d)")
                        v.tensor_tensor(xt, xt, MB[:, 0:D], ALU.add).then_inc(misc_free, 1)
                    elif kind == "S":
                        _, nb, n, h = task
                        i = HG * n + h
                        w = (n % QT + 1) * P
                        dve.wait_ge(s_ps, (b + nb) * NS + (i + 1))
                        if i >= 4 or plan is not FIRST:
                            dve.wait_ge(exp_done, (b + nb) * NS + (i - 3))
                        apart(dve)
                        v.tensor_tensor_reduce(out=negs[:, h, 0:w], in0=S_BANK[i % 2][:, 0:w],
                                               in1=bias_tab[:, HG * (n // QT) + h, SEQ - w:SEQ], scale=-1.0, scalar=3.4e38,
                                               op0=ALU.add, op1=ALU.min,
                                               accum_out=negmax[:, i % 8:i % 8 + 1]).then_inc(s_done, 1)
                    elif kind == "R":
                        _, nb, n = task
                        dve.wait_ge(exp_done, (b + nb) * NS + HG * (n + 1))
                        v.reciprocal(rsum[:, n % 4, :], lsum[:, n % 4, :]).then_inc(rsum_done, 1)
                    elif kind == "L":
                        _, n, jj = task
                        i = blk(n, jj)
                        dve.wait_ge(ph_done, b * NB + (i + 1))
                        v.tensor_tensor(pl[:, i % 3, :], PT_BANK[i % 3][:], ph[:, i % 3, :].bitcast(F32),
                                        ALU.subtract).then_inc(pl_done, 1)

            dve.wait_ge(split_hi, 1)
            v.tensor_tensor(w1s[:, :, 1, :], raw1, w1s[:, :, 0, :].bitcast(F32), ALU.subtract).then_inc(split_lo, 1)
            dve.wait_ge(split_hi, 2)
            v.tensor_tensor(w2s[:, :, :, D:], raw2, w2s[:, :, :, 0:D].bitcast(F32), ALU.subtract).then_inc(split_lo, 1)
            dve.wait_ge(split_hi, 6)
            v.tensor_tensor(wqs[:, 1, :], rawq, wqs[:, 0, :].bitcast(F32), ALU.subtract).then_inc(split_lo, 1)
            for z in range(2):
                v.tensor_tensor(wks[:, 1, z * DH:(z + 1) * DH], rawkv[:, 0:DH], wks[:, 0, 0:DH].bitcast(F32), ALU.subtract).then_inc(split_lo, 1)
            v.tensor_tensor(wvs[:, 1, :], rawkv[:, DH:P], wvs[:, 0, :].bitcast(F32), ALU.subtract).then_inc(split_lo, 1)
            async_done(v.memset(brow[:, SEQ:], MASKED))
            for k, n0, n1 in bucket_runs():
                async_done(v.tensor_scalar(brow[:, SEQ - n1:SEQ - n0], embT[:, k:k + 1].to_broadcast([H, n1 - n0]),
                                           DH ** 0.5, None, ALU.mult))
            waited()
            v.engine_nop().then_inc(brow_done, 1)
            ffn_dve(0)
            if stop > 0:
                dve.wait_ge(combined, TILES)
                layer_norm_stats(1)
                dve.wait_ge(bias_in, 16)
                attention(dve, attention_dve)
            if stop > 1:
                dve.wait_ge(misc_free, MISC_END)
                ffn_dve(1)

        @block.tensor
        def _(pe):
            t_ = nc.tensor
            pe.wait_ge(const_done, 13)
            pe.wait_ge(small_in, 16)

            def three(dst, hi, lo, mh, ml, first=True, last=True):
                t_.matmul(dst, hi, mh, start=first, stop=False)
                t_.matmul(dst, hi, ml, start=False, stop=False)
                return t_.matmul(dst, lo, mh, start=False, stop=last)

            def ffn_pe(r):
                g0 = r * (TILES // 4)
                with pe.Fori(0, TILES // 8) as i:
                    for u in range(2):
                        gi = i * 2 + u
                        pe.wait_ge(xn_done, r * TILES + gi * 4 + 4)
                        for q in range(4):
                            ins = t_.transpose(bank[u][:, q * P:(q + 1) * P], xng[:, u, q, :], ident[:])
                        ins.then_inc(xnT_ps, 1)
                        pe.wait_ge(xnT_sb, g0 + gi + 1)
                        for q in range(4):
                            t_.matmul(bank[2][:, ds((gi * 4 + q) * E, E)], xngT[:, u, q * P:(q + 1) * P], gate_sb[:],
                                      start=True, stop=True).then_inc(logit_ps, 1)
                pe.wait_ge(hot_done, r + 1)
                hot = ohb[:].rearrange("p t e -> p (t e)")
                t_.matmul(bank[3][:, 0:TILES * E], ones_bf[:], hot, start=True, stop=True)
                t_.matmul(bank[4][:, 0:TILES * E], before[:], hot, start=True, stop=True).then_inc(prefix_ps, 1)
                pe.wait_ge(onehot_done, r + 1)
                for c in range(PAIRS):
                    ins = t_.matmul(bank[5][:, 0:2 * ETILES], in_tile[:, c, :], which[:, c, :, :].rearrange("p a b -> p (a b)"),
                                    start=(c == 0), stop=(c == PAIRS - 1))
                ins.then_inc(inv_ps, 1)
                pe.wait_ge(route_done, r + 1)
                if r == 0:
                    pe.wait_ge(split_lo, 2)
                k0 = r * ETILES

                def step(k, s, i, loop=False):
                    if on(k, 2, loop):
                        q = (s - 2) % 2
                        pe.wait_ge(gathered[(s - 2) % 4], dmas(r, i, s - 2))
                        if loop or k >= 4:
                            pe.wait_ge(xl_done, k0 + k - 3)
                        t_.transpose(bank[q][:, 0:P], xr[:, (s - 2) % 4, :], ident[:]).then_inc(xrT_ps, 1)
                    if on(k, 3, loop):
                        q = (s - 3) % 2
                        e = pe.value_load(etile[0:1, ds(k - 3, 1)], min_val=0, max_val=E - 1)
                        pe.wait_ge(xl_done, k0 + k - 2)
                        if loop or k >= 5:
                            pe.wait_ge(gelu_done, k0 + k - 4)
                        wh, wl = (w1s[:, ds(e, 1), z, :].rearrange("p a f -> p (a f)") for z in range(2))
                        three(bank[2 + q][:], xh[:, q, :], xl[:, q, :], wh, wl).then_inc(up_ps, 1)
                    if on(k, 4, loop):
                        q = (s - 4) % 2
                        pe.wait_ge(gelu_done, k0 + k - 3)
                        if loop or k >= 6:
                            pe.wait_ge(hl_done, k0 + k - 5)
                        for c in range(FC):
                            ins = t_.transpose(bank[4 + q][:, c * P:(c + 1) * P], hg[:, q, c * P:(c + 1) * P], ident[:])
                        ins.then_inc(hT_ps, 1)
                    if on(k, 5, loop):
                        q = (s - 5) % 2
                        e = pe.value_load(etile[0:1, ds(k - 5, 1)], min_val=0, max_val=E - 1)
                        pe.wait_ge(hl_done, k0 + k - 4)
                        if loop or k >= 7:
                            pe.wait_ge(yo_done, k0 + k - 6)
                        for c in range(FC):
                            w = w2s[:, ds(e, 1), c, :].rearrange("p a d -> p (a d)")
                            t_.matmul(bank[6 + q][:, 0:2 * D], hh[:, q, c * P:(c + 1) * P], w, start=(c == 0), stop=False)
                            ins = t_.matmul(bank[6 + q][:, 0:2 * D], hl[:, q, c * P:(c + 1) * P], w, start=False, stop=(c == FC - 1))
                        ins.then_inc(y_ps, 1)

                expert_steps(pe, step)

            def attention_pe(plan, b):
                for task, m, _ in walk(plan, b):
                    kind = task[0]
                    if kind == "xT":
                        pe.wait_ge(xa_done, (b + (task[1] + 1)) * QT)
                    if kind in USERS and not (kind == "xT" and plan is FIRST):
                        pe.wait_ge(misc_free, m)
                    if kind == "xT":
                        for q in range(QT):
                            ins = t_.transpose(MB[:, q * P:(q + 1) * P], xa[:, q, :], ident[:])
                    elif kind == "K":
                        ins = three(MB[:], wks[:, 0, :], wks[:, 1, :], xTh[:], xTl[:])
                    elif kind == "V":
                        for q in range(QT):
                            c = slice(q * P, (q + 1) * P)
                            ins = three(MB[:, q * DH:(q + 1) * DH], xTh[:, c], xTl[:, c], wvs[:, 0, :], wvs[:, 1, :])
                    elif kind == "Q":
                        _, _, g, c = task
                        c = slice((2 * g + c) * P, (2 * g + c + 1) * P)
                        ins = three(MB[:], wqs[:, 0, c], wqs[:, 1, c], xTh[:], xTl[:])
                    elif kind == "Y":
                        n = task[1]
                        pe.wait_ge(ot_done, b * NU + (n + 1))
                        for h in range(HG):
                            ins = t_.matmul(MB[:, 0:D], ot[:, n % 2, h * P:(h + 1) * P], wo_sb[:, HG * (n // QT) + h, :],
                                            start=(h == 0), stop=(h == HG - 1))
                    if kind in USERS:
                        ins.then_inc(misc_ps, 1)
                    elif kind == "S":
                        _, nb, n, h = task
                        g, t = divmod(n, QT)
                        i = HG * n + h
                        w = max((t + 1) * P, 256)
                        if t == 0 and h == 0:
                            users = [("Q", nb, g, 1)] + ([("K", nb)] if g == 0 else [])
                            last = max(plan.index(x) for x in users)
                            pe.wait_ge(misc_free, place_of(plan, b, plan[last]))
                        if i >= 2 or plan is not FIRST:
                            pe.wait_ge(s_done, (b + nb) * NS + (i - 1))
                        q = qst[:, g % 2, h, t * P:(t + 1) * P]
                        t_.matmul(S_BANK[i % 2][:, 0:w], q, kst[:, 0, 0:w], start=True, stop=False)
                        t_.matmul(S_BANK[i % 2][:, 0:w], q, kst[:, 1, 0:w], start=False, stop=True).then_inc(s_ps, 1)
                    elif kind == "T":
                        _, n, jj = task
                        i = blk(n, jj)
                        if jj == 0:
                            pe.wait_ge(norm_done, b * NU + (n + 1))
                        if i >= 3:
                            pe.wait_ge(pl_done, b * NB + (i - 2))
                        for h in range(HG):
                            ins = t_.transpose(PT_BANK[i % 3][:, h * P:(h + 1) * P], prob[n % QT][:, h, jj * P:(jj + 1) * P], ident[:])
                        ins.then_inc(pt_ps, 1)
                    elif kind == "AV":
                        _, n, jj = task
                        i = blk(n, jj)
                        pe.wait_ge(pl_done, b * NB + (i + 1))
                        if jj == 0 and n >= 2:
                            pe.wait_ge(ot_done, b * NU + (n - 1))
                        t_.matmul(OT_BANK[n % 2][:], vst[:, jj, :], ph[:, i % 3, :], start=(jj == 0), stop=False)
                        t_.matmul(OT_BANK[n % 2][:], vst[:, jj, :], pl[:, i % 3, :], start=False, stop=(jj == n % QT)).then_inc(av_ps, 1)

            ffn_pe(0)
            if stop > 0:
                pe.wait_ge(split_lo, 6)
                pe.wait_ge(wa_in, 96)
                attention(pe, attention_pe)
            if stop > 1:
                ffn_pe(1)


_INS = ["L0_attn_x", "L0_attn_Wq", "L0_attn_Wkv", "L0_attn_Wout", "L0_attn_bout", "L0_attn_rel_emb",
        "L0_ffn_gate_w", "L0_ffn_fc_w", "L0_ffn_proj_w"]


def kernel(**inputs):
    import concourse.bacc as bacc
    from concourse.bass_utils import run_bass_kernel_spmd

    nc = bacc.Bacc("TRN2", target_bir_lowering=False, num_devices=1)
    arrays, args = {}, []
    for name in _INS:
        a = np.ascontiguousarray(inputs[name])
        arrays[name] = a
        args.append(nc.dram_tensor(name, a.shape, mybir.dt.from_np(a.dtype), kind="ExternalInput").ap())
    args.append(nc.dram_tensor("out", (BATCH, SEQ, D), F32, kind="ExternalOutput").ap())
    build(nc, *args)
    r = run_bass_kernel_spmd(nc, [arrays], core_ids=[0])
    return r.results[0]["out"]
```

```python
from contextlib import ExitStack

import math

import numpy as np

import concourse.bass as bass
from concourse import mybir

P = 128
D = 128
BATCH, SEQ = 8, 512
TILES = BATCH * SEQ // P
E, TOPK, F = 8, 2, 512
FC = F // P
ETILES = TILES * TOPK + E
PAIRS = TILES * TOPK
H, DH = 16, 64
HG, NG = 4, 4
QT = SEQ // P
BUCKETS, MAX_DISTANCE = 32, 128
RING = 3
EPS = 1e-5
MASKED = -3.0e38

LAG_AV, LAG_Y, LAG_R = 2.0, 0.9, 0.6
LEAD, TAIL, S_FIX, K_AT, K_GAP, Q_AT, Q0_AT, Q_GAP, XT_AT, LN_AT, V_AT = 7.0, 2.0, 1.1, 0.5, 1.4, -2.1, 2.0, 1.1, 1.1, 6.4, -2.0
LATER = {("S", "act"): 0.6, ("T", "dve"): 1.15, ("T", "act"): 0.2, ("Y", "dve"): 0.3, ("S", "dve"): 0.1,
         ("R", "dve"): 0.1, ("R", "pool"): 0.5, ("O", "act"): -0.25, ("xT", "act"): 0.3, ("K", "act"): 0.3,
         ("V", "act"): 0.3, ("Q", "act"): 0.3, ("xT", "dve"): 0.7, ("K", "dve"): 0.7, ("V", "dve"): 0.7,
         ("Q", "dve"): 0.7}

F32 = mybir.dt.float32
F32R = mybir.dt.float32r
BF16 = mybir.dt.bfloat16
I32 = mybir.dt.int32
ALU = mybir.AluOpType
ACT = mybir.ActivationFunctionType
AX = mybir.AxisListType.X
ds = bass.ds


def bucket(n):
    exact = BUCKETS // 2
    if n < exact:
        return n
    large = exact + int(math.log(n / exact) / math.log(MAX_DISTANCE / exact) * (BUCKETS - exact))
    return min(large, BUCKETS - 1)


def bucket_runs():
    runs = []
    for n in range(SEQ):
        if runs and runs[-1][0] == bucket(n):
            runs[-1][2] = n + 1
        else:
            runs.append([bucket(n), n, n + 1])
    return runs


def build(nc, x, Wq, Wkv, Wout, bout, rel_emb, gate_w, fc_w, proj_w, out, stop=99):
    ctx = ExitStack()
    with ctx:
        def sb(name, shape, dt=F32):
            return ctx.enter_context(nc.sbuf_tensor(name, shape, dt))

        def sem(name):
            return ctx.enter_context(nc.semaphore(name))

        xn_dram = [nc.dram_tensor(f"xn_dram{r}", [TILES * P, D], F32).ap() for r in range(2)]
        y2_dram = [nc.dram_tensor(f"y2_dram{r}", [TILES * P * TOPK, D], F32).ap() for r in range(2)]
        ROW = SEQ + P
        bias_dram = nc.dram_tensor("bias_dram", [H, P, ROW], F32).ap()

        x_sb = sb("x_sb", [P, TILES, D])
        ident = sb("ident", [P, P])
        ones_bf = sb("ones_bf", [P, P], BF16)
        before = sb("before", [P, P], BF16)
        iota_p = sb("iota_p", [P, P])
        pair_val = sb("pair_val", [P, TOPK])
        tile_val = sb("tile_val", [P, PAIRS])
        rev8 = sb("rev8", [P, E])
        tile_start = sb("tile_start", [P, ETILES])
        gate_sb = sb("gate_sb", [P, E])
        w1s = sb("w1s", [P, E, 2, F], F32R)
        w2s = sb("w2s", [P, E, FC, 2 * D], F32R)
        wqs = sb("wqs", [P, 2, H * DH], F32R)
        wks = sb("wks", [P, 2, P], F32R)
        wvs = sb("wvs", [P, 2, DH], F32R)
        wo_sb = sb("wo_sb", [P, H, D])
        bout_sb = sb("bout_sb", [P, D])
        bias_tab = sb("bias_tab", [P, H, SEQ])
        stats = sb("stats", [P, TILES, 6])
        lnt = sb("lnt", [P, 6, TILES])
        mean = sb("mean", [P, TILES])
        rstd = sb("rstd", [P, TILES])
        gw1 = sb("gw1", [P, TILES])
        gw2 = sb("gw2", [P, TILES])
        eps_t = sb("eps_t", [P, 1])
        base = nc.sbuf_base

        raw1 = bias_tab[:, 0:E, :]
        raw2 = bias_tab[:, E:2 * E, :].rearrange("p e (c d) -> p e c d", c=FC)

        ffn = ExitStack()
        with ffn:
            def fb(name, shape, dt=F32):
                return ffn.enter_context(nc.sbuf_tensor(name, shape, dt))

            yo = fb("yo", [P, 4, D])
            xngT = fb("xngT", [P, 2, 4 * P])
            lg = fb("lg", [P, TILES, E])
            lg2 = fb("lg2", [P, TILES, E])
            eq = fb("eq", [P, TILES, E])
            oh = fb("oh", [P, TOPK, TILES, E])
            ohb = fb("ohb", [P, TILES, E], BF16)
            top = fb("top", [P, 4, TILES])
            scan = fb("scan", [P, 2, 16 + TILES, E])
            cnt = fb("cnt", [P, E])
            cnti = fb("cnti", [P, E], I32)
            padded = fb("padded", [P, E])
            escan = fb("escan", [P, 2, 4 + E])
            ends = fb("ends", [P, E])
            place = lg2
            pos = fb("pos", [P, PAIRS])
            posi = fb("posi", [P, 2, PAIRS], I32)
            posf = fb("posf", [P, 2, PAIRS])
            tilef = fb("tilef", [P, PAIRS])
            in_tile = fb("in_tile", [P, PAIRS, P], BF16)
            which = fb("which", [P, PAIRS, 2, ETILES], BF16)
            inv = fb("inv", [P, 2, ETILES])
            invt = fb("invt", [P, 2, ETILES])
            sidx = fb("sidx", [P, ETILES], I32)
            gidx = fb("gidx", [P, ETILES], I32)
            etf = fb("etf", [P, ETILES])
            etile = fb("etile", [P, ETILES], I32)
            wtmp = fb("wtmp", [P, 2, TILES])
            gring = fb("gring", [P, 4], I32)
            sring = fb("sring", [P, 4], I32)
            xr = fb("xr", [P, 4, D])
            xh = fb("xh", [P, 2, P], F32R)
            xl = fb("xl", [P, 2, P], F32R)
            hg = fb("hg", [P, 2, F])
            ecmp = hg[:].rearrange("p a f -> p (a f)")[:, 0:ETILES * E].rearrange("p (t e) -> p t e", e=E)
            hh = fb("hh", [P, 2, F], F32R)
            hl = fb("hl", [P, 2, F], F32R)
            yt = fb("yt", [P, 2, D])
            xn = in_tile[:].bitcast(F32).rearrange("p a b -> p (a b)").rearrange("p (t d) -> p t d", d=D)
            yc = in_tile[:].bitcast(F32).rearrange("p a b -> p (a b)").rearrange(
                "p (u q d) -> p u q d", u=4, q=4)
            rawq = which[:, 0:28, :, :].bitcast(F32).rearrange("p a b c -> p (a b c)")[:, 0:H * DH]
            rawkv = xr[:, 0, :]
            embT = fb("embT", [H, BUCKETS])
            brow = hg[0:H, :, :].rearrange("p a f -> p (a f)")[:, 0:SEQ + P]
        att = ExitStack()
        with att:
            def ab(name, shape, dt=F32):
                return att.enter_context(nc.sbuf_tensor(name, shape, dt))

            xa = ab("xa", [P, QT, D])
            xTh = ab("xTh", [P, SEQ], F32R)
            xTl = ab("xTl", [P, SEQ], F32R)
            kst = ab("kst", [P, 2, SEQ], F32R)
            vst = ab("vst", [P, QT, 2 * DH], F32R)
            qst = ab("qst", [P, 2, HG, SEQ], F32R)
            prob = [ab(f"prob{t}", [P, HG, (t + 1) * P]) for t in range(QT)]
            negmax = ab("negmax", [P, 8])
            lsum = ab("lsum", [P, 4, HG])
            rsum = ab("rsum", [P, 4, HG])
            ph = ab("ph", [P, RING, HG * P], F32R)
            pl = ab("pl", [P, RING, HG * P], F32R)
            ot = ab("ot", [P, 2, HG * P])

        bank = [ctx.enter_context(nc.psum_tensor(f"bank{i}", [P, 512], F32)) for i in range(8)]

        x_in = [sem(f"x_in{i}") for i in range(4)]
        w1_in, w2_in, wa_in, small_in = sem("w1_in"), sem("w2_in"), sem("wa_in"), sem("small_in")
        const_done, split_hi, split_lo = sem("const_done"), sem("split_hi"), sem("split_lo")
        brow_done, brow_out, bias_in = sem("brow_done"), sem("brow_out"), sem("bias_in")
        dstep = sem("dstep")
        vstep = [0]
        ln_ln = sem("ln_ln")
        ln_var = sem("ln_var")
        ln_done = sem("ln_done")
        xn_done, xnT_ps, xnT_sb, logit_ps = (sem(n) for n in ("xn_done", "xnT_ps", "xnT_sb", "logit_ps"))
        place_done, tiles_done, pool_onehot = sem("place_done"), sem("tiles_done"), sem("pool_onehot")
        xn_out = sem("xn_out")
        gathered = [sem(f"gathered{i}") for i in range(4)]
        scattered = [sem(f"scattered{i}") for i in range(4)]
        lg_diff, lg_exp, hot_done, prefix_ps, onehot_done, inv_ps, route_done = (
            sem(n) for n in ("lg_diff", "lg_exp", "hot_done", "prefix_ps", "onehot_done", "inv_ps", "route_done"))
        gring_done, xrT_ps, xh_done, xl_done, up_ps, gelu_done, hT_ps, hh_done, hl_done, y_ps, yt_done, yo_done = (
            sem(n) for n in ("gring_done", "xrT_ps", "xh_done", "xl_done", "up_ps", "gelu_done", "hT_ps",
                             "hh_done", "hl_done", "y_ps", "yt_done", "yo_done"))
        y2_in = [sem(f"y2_in{i}") for i in range(4)]
        out_done = sem("out_done")
        comb1, combined = sem("comb1"), sem("combined")
        weights_done, pool_comb, pool_combined = sem("weights_done"), sem("pool_comb"), sem("pool_combined")
        xa_done, misc_ps, misc_hi, misc_free, proj_ps, proj_done, s_ps, s_done, exp_done, rsum_done, norm_done = (
            sem(n) for n in ("xa_done", "misc_ps", "misc_hi", "misc_free", "proj_ps", "proj_done", "s_ps", "s_done", "exp_done",
                             "rsum_done", "norm_done"))
        pt_ps, ph_done, pl_done, av_ps, bout_done, ot_done = (
            sem(n) for n in ("pt_ps", "ph_done", "pl_done", "av_ps", "bout_done", "ot_done"))

        block = ctx.enter_context(nc.Block())

        LAST = ETILES + 6
        MAIN0 = 8
        assert (ETILES - MAIN0) % 4 == 0

        def expert_steps(eng, step):
            for k in range(MAIN0):
                step(k, k, 0)
            with eng.Fori(0, (ETILES - MAIN0) // 4) as i:
                for u in range(4):
                    step(i * 4 + (MAIN0 + u), MAIN0 + u, i, loop=True)
            for k in range(ETILES, LAST):
                step(k, k, 0)

        carriers = {}

        def apart(eng):
            eng.reg_alu(carriers[eng], carriers[eng], 1, op=ALU.bitwise_and)

        def carrier(eng):
            carriers[eng] = eng.alloc_register("carrier")
            eng.reg_mov(carriers[eng], 1)

        def carried(eng):
            eng.wait_ge(const_done, carriers[eng])

        def dmas(r, i, s):
            return (i + (r * ETILES // 4 + s // 4 + 1)) * 16

        def on(k, lag, loop):
            return loop or 0 <= k - lag < ETILES

        def attention_plan():
            start = [(n // QT) * (QT * (QT + 1) // 2) + (n % QT) * (n % QT + 1) // 2 for n in range(NG * QT)]
            group = QT * (QT + 1) // 2
            period = NG * group + TAIL
            plan = [(V_AT, ("V", 0))]
            for n, at in enumerate(start):
                t = n % QT
                for jj in range(t + 1):
                    plan.append((at + jj, ("T", n, jj)))
                    plan.append((at + jj + LAG_AV, ("AV", n, jj)))
                plan.append((at + t + LAG_AV + 0.01, ("O", n)))
                plan.append((at + t + LAG_AV + LAG_Y, ("Y", n)))

            def lead(at, task):
                plan.append((at + period, (task[0], 1) + task[2:]) if at < 0 else (at, task))

            lead(2 * group - LEAD + LN_AT - period, ("LN", 0))
            lead(3 * group - LEAD + XT_AT - period, ("xT", 0))
            for g in range(NG):
                for c in range(2):
                    at = g * group - LEAD + Q_AT + Q_GAP * c if g else 3 * group - LEAD + Q0_AT + Q_GAP * c - period
                    lead(at, ("Q", 0, g, c))
            lead(-LEAD + K_AT, ("K", 0))
            weight = [S_FIX + (t + 1) for t in range(QT)]
            for g in range(NG):
                a, z = g * group - LEAD + (K_GAP if g == 0 else 0), (g + 1) * group - LEAD
                for t in range(QT):
                    for h in range(HG):
                        done = sum(weight[:t]) + weight[t] * (h + 0.5) / HG
                        lead(a + (z - a) * done / sum(weight), ("S", 0, g * QT + t, h))
                    lead(a + (z - a) * sum(weight[:t + 1]) / sum(weight) + LAG_R, ("R", 0, g * QT + t))
            return sorted(plan, key=lambda x: x[0])

        def prologue_plan(plan):
            ahead = [x for _, x in plan if x[0] in AHEAD and x[1] == 1]
            return [(float(i), (x[0], 0) + x[2:]) for i, x in enumerate(ahead)]

        AHEAD = ("LN", "xT", "K", "Q", "S", "R")
        PLAN = attention_plan()
        FIRST = prologue_plan(PLAN)
        FINAL = [x for x in PLAN if not (x[1][0] in AHEAD and x[1][1] == 1)]
        USERS = ("xT", "K", "V", "Q")
        HIGHS = {"xT": 1, "K": 1, "V": 1, "Q": 2}

        def tally(plan):
            m = hi = 0
            out = []
            for _, x in plan:
                out.append((m, hi))
                if x[0] in USERS:
                    m, hi = m + 1, hi + HIGHS[x[0]]
            return out, m, hi

        TALLY, NM, NHI = tally(PLAN)
        _, PRE, PREHI = tally(FIRST)
        NS = NG * QT * HG
        NU = NG * QT
        NB = NG * QT * (QT + 1) // 2

        def walk(plan, b, engine):
            counts, _, _ = tally(plan)
            order = sorted(range(len(plan)), key=lambda i: plan[i][0] + LATER.get((plan[i][1][0], engine), 0.0))
            for i in order:
                m, hi = counts[i]
                yield plan[i][1], (m if plan is FIRST else b * NM + (PRE + m)), (hi if plan is FIRST else b * NHI + (PREHI + hi))

        def place_of(plan, b, task):
            m = tally(plan)[0][[x for _, x in plan].index(task)][0] + 1
            return m if plan is FIRST else b * NM + (PRE + m)

        FRONTS = 3
        FRONT_BANK = [bank[0], bank[1], bank[7]]
        PT_BANK = [bank[2], bank[3], bank[4]]
        OT_BANK = [bank[5], bank[6]]

        def fronts(plan):
            return [x for _, x in plan if x[0] in USERS + ("S",)]

        assert len(fronts(PLAN)) % FRONTS == 0
        assert all(x[:2] == ("S", 1) for x in fronts(PLAN)[-FRONTS:])

        def front_bank(plan, task):
            turn = fronts(plan).index(task)
            return FRONT_BANK[(turn - len(fronts(plan)) if plan is FIRST else turn) % FRONTS]

        def front_free(plan, b, task):
            turn = fronts(plan).index(task) - FRONTS
            if turn < 0 and plan is FIRST:
                return None
            kind, nb, *rest = fronts(plan)[turn] if turn >= 0 else ("S", 0, *fronts(PLAN)[turn][2:])
            if kind == "S":
                return s_done, (b + nb) * NS + (HG * rest[0] + rest[1] + 1)
            return misc_free, place_of(plan, b, (kind, nb, *rest))

        def attention(eng, run):
            run(FIRST, 0)
            with eng.Fori(0, BATCH - 1) as b:
                run(PLAN, b)
            run(FINAL, BATCH - 1)

        def blk(n, jj):
            g, t = divmod(n, QT)
            return g * (QT * (QT + 1) // 2) + t * (t + 1) // 2 + jj


        @block.sync
        def _(sp):
            xt = x.rearrange("b (t p) d -> p (b t) d", p=P)
            sp.dma_start(x_sb[:, 0:8, :], xt[:, 0:8, :]).then_inc(x_in[0], 16)
            sp.dma_start(gate_sb[:], gate_w).then_inc(small_in, 16)
            for i in range(1, 4):
                sp.dma_start(x_sb[:, 8 * i:8 * i + 8, :], xt[:, 8 * i:8 * i + 8, :]).then_inc(x_in[i], 16)
            sp.dma_start(raw1, fc_w.rearrange("e d f -> d e f")).then_inc(w1_in, 16)
            sp.dma_start(raw2, proj_w.rearrange("e (c p) d -> p e c d", p=P)).then_inc(w2_in, 16)
            def bias_sp():
                sp.wait_ge(brow_done, 1)
                sp.dma_start(bias_dram, brow.unsqueeze(1).to_broadcast([H, P, ROW])).then_inc(brow_out, 16)
                sp.wait_ge(brow_out, 16)
                sp.wait_ge(split_lo, 6)
                src = bass.AP(tensor=bias_dram.tensor, offset=bias_dram.offset + P - 1,
                              ap=[[ROW - 1, P], [P * ROW, H], [1, SEQ]])
                sp.dma_start(bias_tab[:], src).then_inc(bias_in, 16)

            def ffn_sp(r):
                xd = xn_dram[r].rearrange("(t p) d -> p t d", p=P)
                with sp.Fori(0, TILES // 8) as i:
                    sp.wait_ge(xn_done, i * 8 + (r * TILES + 8))
                    sp.dma_start(xd[:, ds(i * 8, 8), :], xn[:, ds(i * 8, 8), :]).then_inc(xn_out, 16)
                if r == 0:
                    bias_sp()
                for s in range(4):
                    sp.wait_ge(scattered[s], 4 * ETILES * (r + 1))
                yd = y2_dram[r].rearrange("(t p k) d -> p t (k d)", p=P, k=TOPK)
                for gi in range(4):
                    sp.dma_start(yc[:, gi, :, :], yd[:, 4 * gi:4 * gi + 4, :]).then_inc(y2_in[gi], 16)
                for gi in range(4, TILES // 4):
                    if gi % 4 == 3:
                        sp.wait_ge(pool_combined, r * (TILES // 16) + gi // 4)
                    else:
                        sp.wait_ge(combined, r * (TILES * 3 // 4) + (gi - 3) * 4)
                    sp.dma_start(yc[:, gi - 4, :, :], yd[:, 4 * gi:4 * gi + 4, :]).then_inc(y2_in[gi - 4], 16)

            ffn_sp(0)
            if stop > 1:
                ffn_sp(1)
            od = out.rearrange("b (t p) d -> p (b t) d", p=P)
            for gi in range(TILES // 4):
                if stop == 1:
                    sp.wait_ge(proj_done, BATCH * NU)
                else:
                    r = 1 if stop > 1 else 0
                    if gi % 4 == 3:
                        sp.wait_ge(pool_combined, r * (TILES // 16) + gi // 4 + 1)
                    else:
                        sp.wait_ge(combined, r * (TILES * 3 // 4) + (gi - gi // 4 + 1) * 4)
                sp.dma_start(od[:, 4 * gi:4 * gi + 4, :], x_sb[:, 4 * gi:4 * gi + 4, :]).then_inc(out_done, 16)
            sp.wait_ge(out_done, 16 * (TILES // 4))

        @block.gpsimd
        def _(gp):
            g = nc.gpsimd
            carrier(gp)
            g.memset(ident[:], 0.0).then_inc(const_done, 1)
            g.memset(before[:], 1.0).then_inc(const_done, 1)
            g.memset(ones_bf[:], 1.0).then_inc(const_done, 1)
            gp.wait_ge(const_done, 3)
            g.affine_select(out=ident[:], in_=ident[:], compare_op=ALU.not_equal, fill=1.0,
                            base=0, pattern=[[-1, P]], channel_multiplier=1).then_inc(const_done, 1)
            g.affine_select(out=before[:], in_=before[:], compare_op=ALU.is_gt, fill=0.0,
                            base=0, pattern=[[1, P]], channel_multiplier=-1).then_inc(const_done, 1)
            iota = dict(allow_small_or_imprecise_dtypes=True)
            g.iota(iota_p[:], pattern=[[1, P]], base=0, channel_multiplier=0, **iota).then_inc(const_done, 1)
            g.iota(pair_val[:], pattern=[[1, TOPK]], base=1, channel_multiplier=2, **iota).then_inc(const_done, 1)
            g.iota(tile_val[:], pattern=[[0, TOPK], [1, TILES]], base=0, channel_multiplier=0, **iota).then_inc(const_done, 1)
            g.iota(rev8[:], pattern=[[-1, E]], base=E, channel_multiplier=0, **iota).then_inc(const_done, 1)
            g.iota(tile_start[:], pattern=[[P, ETILES]], base=0, channel_multiplier=0, **iota).then_inc(const_done, 1)
            g.memset(eps_t[:], EPS).then_inc(const_done, 1)
            g.memset(scan[:, :, 0:17, :], 0.0).then_inc(const_done, 1)
            g.memset(escan[:, :, 0:5], 0.0).then_inc(const_done, 1)
            g.dma_start(rawq, Wq).then_inc(wa_in, 16)
            g.dma_start(rawkv, Wkv).then_inc(wa_in, 16)
            for z in range(2):
                g.dma_start(wo_sb[z * DH:(z + 1) * DH, :, :], Wout.rearrange("(h p) d -> p h d", p=DH)).then_inc(wa_in, 16)
            g.dma_start(embT[:], rel_emb.rearrange("k h -> h k"), allow_slow_non_contiguous=True).then_inc(wa_in, 16)
            g.dma_start(bout_sb[:], bout.rearrange("(a d) -> a d", a=1).to_broadcast([P, D])).then_inc(wa_in, 16)

            gp.wait_ge(wa_in, 96)
            gp.wait_ge(split_hi, 4)
            for low, raw, high in ((wqs[:, 1, :], rawq, wqs[:, 0, :]),
                                   (wks[:, 1, 0:DH], rawkv[:, 0:DH], wks[:, 0, 0:DH]),
                                   (wks[:, 1, DH:P], rawkv[:, 0:DH], wks[:, 0, 0:DH]),
                                   (wvs[:, 1, :], rawkv[:, DH:P], wvs[:, 0, :])):
                g.tensor_tensor(out=low, in0=raw, in1=high.bitcast(F32), op=ALU.subtract).then_inc(split_lo, 1)
            gp.wait_ge(split_hi, 5)
            g.tensor_tensor(out=w1s[:, :, 1, :], in0=raw1, in1=w1s[:, :, 0, :].bitcast(F32), op=ALU.subtract).then_inc(split_lo, 1)
            gp.wait_ge(split_hi, 6)
            g.tensor_tensor(out=w2s[:, :, :, D:], in0=raw2, in1=w2s[:, :, :, 0:D].bitcast(F32), op=ALU.subtract).then_inc(split_lo, 1)

            def ffn_pool(r):
                k0 = r * ETILES
                if r:
                    gp.wait_ge(proj_done, BATCH * NU)
                    g.memset(scan[:, :, 0:17, :], 0.0).then_inc(const_done, 1)
                    g.memset(escan[:, :, 0:5], 0.0).then_inc(const_done, 1)
                gp.wait_ge(tiles_done, r + 1)
                g.tensor_tensor(out=which[:, TILES:, 1, :], in0=which[:, TILES:, 0, :],
                                in1=tile_val[:, TILES:].unsqueeze(2).to_broadcast([P, TILES, ETILES]),
                                op=ALU.mult).then_inc(pool_onehot, 1)
                gp.wait_ge(xn_out, 64 * (r + 1))
                gp.wait_ge(route_done, r + 1)

                def step(k, s, i, loop=False):
                    if on(k, 0, loop):
                        gp.wait_ge(gring_done, k0 + k + 1)
                        if loop or k >= 4:
                            gp.wait_ge(xrT_ps, k0 + k - 3)
                        apart(gp)
                        g.indirect_dma_start(out=xr[:, s % 4, :], out_offset=None, in_=xn_dram[r],
                                             in_offset=bass.IndirectOffsetOnAxis(ap=gring[:, s % 4:s % 4 + 1], axis=0),
                                             ).then_inc(gathered[s % 4], 16)
                    if on(k, 6, loop):
                        gp.wait_ge(yo_done, k0 + k - 5)
                        q = (s - 6) % 4
                        apart(gp)
                        g.indirect_dma_start(out=y2_dram[r], in_=yo[:, q, :], in_offset=None,
                                             out_offset=bass.IndirectOffsetOnAxis(ap=sring[:, q:q + 1], axis=0),
                                             bounds_check=TILES * P * TOPK - 1, oob_is_err=False).then_inc(scattered[q], 16)

                expert_steps(gp, step)
                gp.wait_ge(weights_done, r + 1)
                for i in range(TILES // 16):
                    own = slice(i * 16 + 12, i * 16 + 16)
                    gp.wait_ge(y2_in[3], (i + r * (TILES // 16) + 1) * 16)
                    for c, w in ((0, gw1), (1, gw2)):
                        part = yc[:, 3, :, c * D:(c + 1) * D]
                        g.tensor_tensor(out=part, in0=part, in1=w[:, own].unsqueeze(2).to_broadcast([P, 4, D]),
                                        op=ALU.mult).then_inc(pool_comb, 1)
                    for c in range(TOPK):
                        gp.wait_ge(pool_comb, (r * (TILES // 16) + i) * 3 + 2 + c)
                        g.tensor_tensor(out=x_sb[:, own, :], in0=x_sb[:, own, :], in1=yc[:, 3, :, c * D:(c + 1) * D],
                                        op=ALU.add).then_inc(pool_comb if c == 0 else pool_combined, 1)

            ffn_pool(0)
            if stop > 0:
                def run(plan, b):
                    for task, _, _ in walk(plan, b, "pool"):
                        if task[0] == "LN":
                            gp.wait_ge(xa_done, (b + (task[1] + 1)) * QT)
                            xb = x_sb[:, ds((b + task[1]) * QT, QT), :]
                            g.tensor_tensor(out=xb, in0=xb, in1=bout_sb[:].unsqueeze(1).to_broadcast([P, QT, D]),
                                            op=ALU.add).then_inc(bout_done, 1)
                        elif task[0] == "R":
                            _, nb, n = task
                            gp.wait_ge(rsum_done, (b + nb) * NU + (n + 1))
                            pv = prob[n % QT][:]
                            g.tensor_tensor(out=pv, in0=pv, in1=rsum[:, n % 4, :].unsqueeze(2).to_broadcast([P, HG, (n % QT + 1) * P]),
                                            op=ALU.mult).then_inc(norm_done, 1)

                attention(gp, run)
            if stop > 1:
                ffn_pool(1)
            carried(gp)

        @block.scalar
        def _(act):
            a = nc.scalar

            def ln_act(r):
                act.wait_ge(const_done, 13)
                act.wait_ge(ln_var, r + 1)
                a.activation(lnt[:, 3, :], lnt[:, 2, :], ACT.Ln, bias=eps_t[:, 0:1]).then_inc(ln_ln, 1)
                act.wait_ge(ln_ln, 2 * r + 1)
                a.activation(lnt[:, 4, :], lnt[:, 3, :], ACT.Exp, scale=-0.5).then_inc(ln_ln, 1)

            def ffn_act(r):
                ln_act(2 * r)
                with act.Fori(0, TILES // 8) as i:
                    for u in range(2):
                        act.wait_ge(xnT_ps, r * (TILES // 4) + i * 2 + (u + 1))
                        a.activation(xngT[:, u, :], bank[u][:], ACT.Copy).then_inc(xnT_sb, 1)
                if r == 0:
                    act.wait_ge(wa_in, 96)
                    a.activation(wqs[:, 0, :], rawq, ACT.Copy).then_inc(split_hi, 1)
                    a.activation(wks[:, 0, 0:DH], rawkv[:, 0:DH], ACT.Copy).then_inc(split_hi, 1)
                    a.activation(wks[:, 0, DH:P], rawkv[:, 0:DH], ACT.Copy).then_inc(split_hi, 1)
                    a.activation(wvs[:, 0, :], rawkv[:, DH:P], ACT.Copy).then_inc(split_hi, 1)
                    act.wait_ge(w1_in, 16)
                    a.activation(w1s[:, :, 0, :], raw1, ACT.Copy).then_inc(split_hi, 1)
                    act.wait_ge(w2_in, 16)
                    a.activation(w2s[:, :, :, 0:D], raw2, ACT.Copy).then_inc(split_hi, 1)
                act.wait_ge(lg_diff, r + 1)
                a.activation(wtmp[:, 1, :], wtmp[:, 0, :], ACT.Exp).then_inc(lg_exp, 1)
                k0 = r * ETILES

                def step(k, s, i, loop=False):
                    if on(k, 2, loop):
                        q = (s - 2) % 2
                        act.wait_ge(xrT_ps, k0 + k - 1)
                        if loop or k >= 4:
                            act.wait_ge(up_ps, k0 + k - 3)
                        a.activation(xh[:, q, :], bank[q][:, 0:P], ACT.Copy).then_inc(xh_done, 1)
                    if on(k, 3, loop):
                        q = (s - 3) % 2
                        act.wait_ge(up_ps, k0 + k - 2)
                        if loop or k >= 5:
                            act.wait_ge(hT_ps, k0 + k - 4)
                        a.activation(hg[:, q, :], bank[2 + q][:], ACT.Gelu).then_inc(gelu_done, 1)
                    if on(k, 4, loop):
                        q = (s - 4) % 2
                        act.wait_ge(hT_ps, k0 + k - 3)
                        if loop or k >= 6:
                            act.wait_ge(y_ps, k0 + k - 5)
                        a.activation(hh[:, q, :], bank[4 + q][:], ACT.Copy).then_inc(hh_done, 1)
                    if on(k, 5, loop):
                        q = (s - 5) % 2
                        act.wait_ge(y_ps, k0 + k - 4)
                        if loop or k >= 7:
                            act.wait_ge(yo_done, k0 + k - 6)
                        a.activation(yt[:, q, :], bank[6 + q][:, D:2 * D], ACT.Copy).then_inc(yt_done, 1)

                expert_steps(act, step)

            def attention_act(plan, b):
                for task, m, hi in walk(plan, b, "act"):
                    kind = task[0]
                    if kind in USERS:
                        front = front_bank(plan, task)
                    if kind in ("xT", "K", "V"):
                        act.wait_ge(misc_ps, m + 1)
                        dst = {"xT": xTh[:], "K": kst[:, 0, :], "V": vst[:, :, 0:DH]}[kind]
                        src = front[:, 0:QT * DH].rearrange("p (t d) -> p t d", d=DH) if kind == "V" else front[:]
                        a.activation(dst, src, ACT.Copy).then_inc(misc_hi, 1)
                    elif kind == "Q":
                        _, _, g, c = task
                        act.wait_ge(misc_ps, m + 1)
                        for o in range(2):
                            a.activation(qst[0:DH, g % 2, 2 * c + o, :], front[DH * o:DH * o + DH, :], ACT.Copy,
                                         scale=DH ** -0.5).then_inc(misc_hi, 1)
                    elif kind == "S":
                        _, nb, n, h = task
                        w = (n % QT + 1) * P
                        act.wait_ge(s_done, (b + nb) * NS + (HG * n + h + 1))
                        a.activation(prob[n % QT][:, h, :], prob[n % QT][:, h, :], ACT.Exp, scale=-1.0,
                                     bias=negmax[:, (HG * n + h) % 8:(HG * n + h) % 8 + 1],
                                     accum_out=lsum[:, n % 4, h:h + 1]).then_inc(exp_done, 1)
                    elif kind == "T":
                        _, n, jj = task
                        i = blk(n, jj)
                        act.wait_ge(pt_ps, b * NB + (i + 1))
                        if i >= RING:
                            act.wait_ge(av_ps, b * NB + (i - RING + 1))
                        a.activation(ph[:, i % RING, :], PT_BANK[i % 3][:], ACT.Copy).then_inc(ph_done, 1)
                    elif kind == "O":
                        n = task[1]
                        act.wait_ge(av_ps, b * NB + (blk(n, n % QT) + 1))
                        if n >= 2:
                            act.wait_ge(proj_ps, b * NU + (n - 1))
                        a.activation(ot[:, n % 2, :], OT_BANK[n % 2][:], ACT.Copy).then_inc(ot_done, 1)

            ffn_act(0)
            if stop > 0:
                ln_act(1)
                attention(act, attention_act)
            if stop > 1:
                ffn_act(1)

        @block.vector
        def _(dve):
            v = nc.vector
            carrier(dve)

            def step_done(ins):
                vstep[0] += 1
                ins.then_inc(dstep, 1)
                dve.wait_ge(dstep, vstep[0])

            def async_done(ins):
                vstep[0] += 1
                ins.then_inc(dstep, 1)

            def waited():
                dve.wait_ge(dstep, vstep[0])

            def layer_norm_stats(r, first=False):
                for t in range(TILES):
                    if first and t % 8 == 0:
                        dve.wait_ge(x_in[t // 8], 16)
                    v.bn_stats(out=stats[:, t, :], in_=x_sb[:, t, :]).then_inc(dstep, 1)
                vstep[0] += TILES
                waited()
                me, m2e, mo, m2o = (stats[:, :, s] for s in (1, 2, 4, 5))
                async_done(v.tensor_tensor(lnt[:, 0, :], me, mo, ALU.add))
                async_done(v.tensor_tensor(lnt[:, 1, :], me, mo, ALU.subtract))
                async_done(v.tensor_tensor(lnt[:, 5, :], m2e, m2o, ALU.add))
                waited()
                async_done(v.tensor_scalar(mean[:], lnt[:, 0, :], 0.5, None, ALU.mult))
                step_done(v.scalar_tensor_tensor(out=lnt[:, 3, :], in0=lnt[:, 1, :], scalar=D / 4.0, in1=lnt[:, 1, :],
                                                 op0=ALU.mult, op1=ALU.mult))
                step_done(v.tensor_tensor(lnt[:, 5, :], lnt[:, 5, :], lnt[:, 3, :], ALU.add))
                v.tensor_scalar(lnt[:, 2, :], lnt[:, 5, :], 1.0 / D, None, ALU.mult).then_inc(ln_var, 1)
                dve.wait_ge(ln_ln, 2 * r + 2)
                y = lnt[:, 4, :]
                step_done(v.tensor_tensor(lnt[:, 0, :], y, y, ALU.mult))
                step_done(v.scalar_tensor_tensor(out=lnt[:, 1, :], in0=lnt[:, 2, :], scalar=EPS, in1=lnt[:, 0, :],
                                                 op0=ALU.add, op1=ALU.mult))
                step_done(v.tensor_scalar(lnt[:, 0, :], lnt[:, 1, :], -0.5, 1.5, ALU.mult, ALU.add))
                step_done(v.tensor_tensor(rstd[:], y, lnt[:, 0, :], ALU.mult))

            def bias_row():
                dve.wait_ge(wa_in, 96)
                async_done(v.memset(brow[:, SEQ:], MASKED))
                for k, n0, n1 in bucket_runs():
                    async_done(v.tensor_scalar(brow[:, SEQ - n1:SEQ - n0], embT[:, k:k + 1].to_broadcast([H, n1 - n0]),
                                               DH ** 0.5, None, ALU.mult))
                waited()
                v.engine_nop().then_inc(brow_done, 1)

            def routing(r):
                bc = lambda t: t.unsqueeze(2).to_broadcast([P, TILES, E])
                dve.wait_ge(logit_ps, (r + 1) * TILES)
                if r:
                    carried(dve)
                step_done(v.tensor_copy(lg[:].rearrange("p t e -> p (t e)"), bank[2][:, 0:TILES * E]))
                rev = rev8[:].unsqueeze(1).to_broadcast([P, TILES, E])
                src = lg
                for c in range(TOPK):
                    step_done(v.tensor_reduce(out=top[:, c, :], in_=src[:], op=ALU.max, axis=AX))
                    step_done(v.tensor_tensor(eq[:], src[:], bc(top[:, c, :]), ALU.is_equal))
                    step_done(v.tensor_tensor(eq[:], eq[:], rev, ALU.mult))
                    step_done(v.tensor_reduce(out=top[:, 2 + c, :], in_=eq[:], op=ALU.max, axis=AX))
                    step_done(v.tensor_tensor(oh[:, c, :, :], rev, bc(top[:, 2 + c, :]), ALU.is_equal))
                    if c == 0:
                        step_done(v.scalar_tensor_tensor(out=lg2[:], in0=oh[:, 0, :, :], scalar=MASKED, in1=lg[:],
                                                         op0=ALU.mult, op1=ALU.add))
                        src = lg2
                v.tensor_tensor(ohb[:], oh[:, 0, :, :], oh[:, 1, :, :], ALU.add).then_inc(hot_done, 1)
                v.tensor_tensor(wtmp[:, 0, :], top[:, 1, :], top[:, 0, :], ALU.subtract).then_inc(lg_diff, 1)
                dve.wait_ge(prefix_ps, r + 1)
                if r:
                    dve.wait_ge(const_done, 15)
                tot = bank[3][:, 0:TILES * E].rearrange("p (t e) -> p t e", e=E)
                step_done(v.tensor_copy(scan[:, 0, 17:16 + TILES, :], tot[:, 0:TILES - 1, :]))
                cur = 0
                for sh in (1, 2, 4, 8, 16):
                    step_done(v.tensor_tensor(scan[:, 1 - cur, 16:, :], scan[:, cur, 16:, :],
                                              scan[:, cur, 16 - sh:16 + TILES - sh, :], ALU.add))
                    cur = 1 - cur
                step_done(v.tensor_tensor(cnt[:], scan[:, cur, 15 + TILES, :], tot[:, TILES - 1, :], ALU.add))
                step_done(v.tensor_scalar(cnti[:], cnt[:], float(P - 1), None, ALU.add))
                step_done(v.tensor_scalar(cnti[:], cnti[:], 7, 7, ALU.logical_shift_right, ALU.logical_shift_left))
                async_done(v.tensor_copy(padded[:], cnti[:]))
                step_done(v.tensor_copy(escan[:, 0, 5:4 + E], cnti[:, 0:E - 1]))
                ec = 0
                for sh in (1, 2, 4):
                    step_done(v.tensor_tensor(escan[:, 1 - ec, 4:], escan[:, ec, 4:], escan[:, ec, 4 - sh:4 + E - sh], ALU.add))
                    ec = 1 - ec
                ebase = escan[:, ec, 4:]
                async_done(v.tensor_tensor(ends[:], ebase, padded[:], ALU.add))
                step_done(v.tensor_tensor(place[:], scan[:, cur, 16:, :], ebase.unsqueeze(1).to_broadcast([P, TILES, E]), ALU.add))
                step_done(v.tensor_tensor(place[:], place[:], bank[4][:, 0:TILES * E].rearrange("p (t e) -> p t e", e=E), ALU.add))
                for c in range(TOPK):
                    step_done(v.tensor_tensor(eq[:], place[:], oh[:, c, :, :], ALU.mult))
                    step_done(v.tensor_reduce(out=pos[:, c * TILES:(c + 1) * TILES], in_=eq[:], op=ALU.add, axis=AX))
                step_done(v.tensor_copy(posi[:, 0, :], pos[:]))
                async_done(v.tensor_scalar(posi[:, 1, :], posi[:, 0, :], 7, None, ALU.logical_shift_right))
                waited()
                step_done(v.tensor_scalar(posi[:, 0, :], posi[:, 0, :], P - 1, None, ALU.bitwise_and))
                v.tensor_copy(posf[:], posi[:]).then_inc(place_done, 1)
                dve.wait_ge(place_done, r + 1)
                dve.wait_ge(xn_out, 64 * (r + 1))
                async_done(v.tensor_tensor(tilef[:], pos[:], posf[:, 0, :], ALU.subtract))
                if r == 0:
                    dve.wait_ge(split_lo, 4)
                waited()
                for c in range(TOPK):
                    own = slice(c * TILES, (c + 1) * TILES)
                    ins = v.tensor_tensor(which[:, own, 0, :], tile_start[:].unsqueeze(1).to_broadcast([P, TILES, ETILES]),
                                          tilef[:, own].unsqueeze(2).to_broadcast([P, TILES, ETILES]), ALU.is_equal)
                    if c == 0:
                        step_done(ins)
                        step_done(v.tensor_tensor(which[:, own, 1, :], which[:, own, 0, :],
                                                  tile_val[:, own].unsqueeze(2).to_broadcast([P, TILES, ETILES]), ALU.mult))
                    else:
                        ins.then_inc(tiles_done, 1)
                    async_done(v.tensor_tensor(in_tile[:, own, :], iota_p[:].unsqueeze(1).to_broadcast([P, TILES, P]),
                                               posf[:, 0, own].unsqueeze(2).to_broadcast([P, TILES, P]), ALU.is_equal))
                    if c:
                        dve.wait_ge(pool_onehot, r + 1)
                    waited()
                    v.tensor_scalar(which[:, own, 0, :], which[:, own, 0, :], pair_val[:, c:c + 1], None,
                                    ALU.mult).then_inc(onehot_done, 1)
                if r == 0:
                    dve.wait_ge(brow_out, 16)
                step_done(v.tensor_tensor(ecmp, tile_start[:].unsqueeze(2).to_broadcast([P, ETILES, E]),
                                          ends[:].unsqueeze(1).to_broadcast([P, ETILES, E]), ALU.is_ge))
                step_done(v.tensor_reduce(out=etf[:], in_=ecmp[:, :, 0:E - 1], op=ALU.add, axis=AX))
                async_done(v.tensor_copy(etile[:], etf[:]))
                dve.wait_ge(lg_exp, r + 1)
                step_done(v.tensor_scalar(wtmp[:, 0, :], wtmp[:, 1, :], 2.0, 2.0, ALU.mult, ALU.add))
                step_done(v.reciprocal(gw1[:], wtmp[:, 0, :]))
                v.tensor_tensor(gw2[:], gw1[:], wtmp[:, 1, :], ALU.mult).then_inc(weights_done, 1)
                dve.wait_ge(weights_done, r + 1)
                dve.wait_ge(inv_ps, r + 1)
                step_done(v.tensor_copy(inv[:].rearrange("p a b -> p (a b)"), bank[5][:, 0:2 * ETILES]))
                step_done(v.scalar_tensor_tensor(out=invt[:, 0, :], in0=inv[:, 1, :], scalar=2.0 * P, in1=inv[:, 0, :],
                                                 op0=ALU.mult, op1=ALU.add))
                step_done(v.tensor_scalar(invt[:, 1, :], invt[:, 0, :], 0.0, 1.0e5, ALU.is_equal, ALU.mult))
                step_done(v.scalar_tensor_tensor(out=inv[:, 0, :], in0=invt[:, 0, :], scalar=-1.0, in1=invt[:, 1, :],
                                                 op0=ALU.add, op1=ALU.add))
                step_done(v.tensor_copy(sidx[:], inv[:, 0, :]))
                step_done(v.tensor_scalar(invt[:, 1, :], invt[:, 0, :], -1.0, 0.0, ALU.add, ALU.max))
                step_done(v.tensor_copy(gidx[:], invt[:, 1, :]))
                v.tensor_scalar(gidx[:], gidx[:], 1, None, ALU.logical_shift_right).then_inc(route_done, 1)
                dve.wait_ge(route_done, r + 1)

            def ffn_dve(r):
                layer_norm_stats(2 * r, first=(r == 0))
                if r == 0:
                    dve.wait_ge(const_done, 13)
                with dve.Fori(0, TILES // 8) as i:
                    for u in range(8):
                        t = i * 8 + u
                        v.tensor_scalar(xn[:, ds(t, 1), :].rearrange("p a d -> p (a d)"),
                                        x_sb[:, ds(t, 1), :].rearrange("p a d -> p (a d)"),
                                        mean[:, ds(t, 1)], rstd[:, ds(t, 1)], ALU.subtract, ALU.mult).then_inc(xn_done, 1)
                if r == 0:
                    bias_row()
                routing(r)
                k0 = r * ETILES

                def step(k, s, i, loop=False):
                    if on(k, 0, loop):
                        if loop or k >= 4:
                            dve.wait_ge(gathered[s % 4], dmas(r, i, s - 4))
                        v.tensor_copy(gring[:, s % 4:s % 4 + 1], gidx[:, ds(k, 1)]).then_inc(gring_done, 1)
                    if on(k, 2, loop):
                        q = (s - 2) % 2
                        dve.wait_ge(xh_done, k0 + k - 1)
                        v.tensor_tensor(xl[:, q, :], bank[q][:, 0:P], xh[:, q, :].bitcast(F32), ALU.subtract).then_inc(xl_done, 1)
                    if on(k, 4, loop):
                        q = (s - 4) % 2
                        dve.wait_ge(hh_done, k0 + k - 3)
                        v.tensor_tensor(hl[:, q, :], bank[4 + q][:], hh[:, q, :].bitcast(F32), ALU.subtract).then_inc(hl_done, 1)
                    if on(k, 5, loop):
                        q = (s - 5) % 2
                        dve.wait_ge(yt_done, k0 + k - 4)
                        if loop or k >= 9:
                            dve.wait_ge(scattered[(s - 5) % 4], dmas(r, i, s - 9))
                        v.tensor_copy(sring[:, (s - 5) % 4:(s - 5) % 4 + 1], sidx[:, ds(k - 5, 1)])
                        v.tensor_tensor(yo[:, (s - 5) % 4, :], bank[6 + q][:, 0:D], yt[:, q, :], ALU.add).then_inc(yo_done, 1)

                expert_steps(dve, step)
                with dve.Fori(0, TILES // 16) as i:
                    for u in range(3):
                        dve.wait_ge(y2_in[u], (i + (r * (TILES // 16) + 1)) * 16)
                        for c, w in ((0, gw1), (1, gw2)):
                            for q in range(4):
                                t = i * 16 + (u * 4 + q)
                                xt = x_sb[:, ds(t, 1), :].rearrange("p a d -> p (a d)")
                                v.scalar_tensor_tensor(out=xt, in0=yc[:, u, q, c * D:(c + 1) * D], scalar=w[:, ds(t, 1)],
                                                       in1=xt, op0=ALU.mult, op1=ALU.add).then_inc(comb1 if c == 0 else combined, 1)
                            if c == 0:
                                dve.wait_ge(comb1, i * 12 + (r * (TILES * 3 // 4) + (u + 1) * 4))

            def attention_dve(plan, b):
                for task, m, hi in walk(plan, b, "dve"):
                    kind = task[0]
                    if kind in USERS + ("S",):
                        front = front_bank(plan, task)
                    if kind == "LN":
                        for q in range(QT):
                            t = (b + task[1]) * QT + q
                            v.tensor_scalar(xa[:, q, :], x_sb[:, ds(t, 1), :].rearrange("p a d -> p (a d)"),
                                            mean[:, ds(t, 1)], rstd[:, ds(t, 1)], ALU.subtract, ALU.mult).then_inc(xa_done, 1)
                    elif kind in ("xT", "K", "V"):
                        dve.wait_ge(misc_hi, hi + 1)
                        hi_t, dst = {"xT": (xTh[:], xTl[:]), "K": (kst[:, 0, :], kst[:, 1, :]),
                                     "V": (vst[:, :, 0:DH], vst[:, :, DH:])}[kind]
                        src = front[:, 0:QT * DH].rearrange("p (t d) -> p t d", d=DH) if kind == "V" else front[:]
                        v.tensor_tensor(dst, src, hi_t.bitcast(F32), ALU.subtract).then_inc(misc_free, 1)
                    elif kind == "Q":
                        _, _, g, c = task
                        for o in range(2):
                            dve.wait_ge(misc_hi, hi + (o + 1))
                            ins = v.scalar_tensor_tensor(out=qst[DH:P, g % 2, 2 * c + o, :], in0=front[DH * o:DH * o + DH, :],
                                                         scalar=DH ** -0.5, in1=qst[0:DH, g % 2, 2 * c + o, :].bitcast(F32),
                                                         op0=ALU.mult, op1=ALU.subtract)
                        ins.then_inc(misc_free, 1)
                    elif kind == "Y":
                        n = task[1]
                        dve.wait_ge(proj_ps, b * NU + (n + 1))
                        if n < QT:
                            dve.wait_ge(bout_done, b + 1)
                        else:
                            dve.wait_ge(proj_done, b * NU + (n - QT + 1))
                        xt = x_sb[:, ds(b * QT + n % QT, 1), :].rearrange("p a d -> p (a d)")
                        v.tensor_tensor(xt, xt, OT_BANK[n % 2][:, 0:D], ALU.add).then_inc(proj_done, 1)
                    elif kind == "S":
                        _, nb, n, h = task
                        i = HG * n + h
                        w = (n % QT + 1) * P
                        dve.wait_ge(s_ps, (b + nb) * NS + (i + 1))
                        if i >= 8 or plan is not FIRST:
                            dve.wait_ge(exp_done, (b + nb) * NS + (i - 7))
                        apart(dve)
                        v.tensor_tensor_reduce(out=prob[n % QT][:, h, :], in0=front[:, 0:w],
                                               in1=bias_tab[:, HG * (n // QT) + h, SEQ - w:SEQ], scale=-1.0, scalar=3.4e38,
                                               op0=ALU.add, op1=ALU.min,
                                               accum_out=negmax[:, i % 8:i % 8 + 1]).then_inc(s_done, 1)
                    elif kind == "R":
                        _, nb, n = task
                        dve.wait_ge(exp_done, (b + nb) * NS + HG * (n + 1))
                        v.reciprocal(rsum[:, n % 4, :], lsum[:, n % 4, :]).then_inc(rsum_done, 1)
                    elif kind == "T":
                        _, n, jj = task
                        i = blk(n, jj)
                        dve.wait_ge(ph_done, b * NB + (i + 1))
                        v.tensor_tensor(pl[:, i % RING, :], PT_BANK[i % 3][:], ph[:, i % RING, :].bitcast(F32),
                                        ALU.subtract).then_inc(pl_done, 1)

            ffn_dve(0)
            if stop > 0:
                dve.wait_ge(combined, TILES * 3 // 4)
                dve.wait_ge(pool_combined, TILES // 16)
                layer_norm_stats(1)
                dve.wait_ge(bias_in, 16)
                attention(dve, attention_dve)
            if stop > 1:
                dve.wait_ge(proj_done, BATCH * NU)
                ffn_dve(1)

        @block.tensor
        def _(pe):
            t_ = nc.tensor
            pe.wait_ge(const_done, 13)
            pe.wait_ge(small_in, 16)

            def three(dst, hi, lo, mh, ml, first=True, last=True):
                t_.matmul(dst, hi, mh, start=first, stop=False)
                t_.matmul(dst, hi, ml, start=False, stop=False)
                return t_.matmul(dst, lo, mh, start=False, stop=last)

            expert = [pe.alloc_register(f"expert{i}") for i in range(4)]

            def expert_of(s):
                return pe.snap(expert[s % 4], min_val=0, max_val=E - 1)

            def ffn_pe(r):
                g0 = r * (TILES // 4)
                def transposes(gi, u):
                    pe.wait_ge(xn_done, r * TILES + gi * 4 + 4)
                    for q in range(4):
                        ins = t_.transpose(bank[u][:, q * P:(q + 1) * P], xn[:, gi * 4 + q, :], ident[:])
                    ins.then_inc(xnT_ps, 1)

                def logits(gi, u):
                    pe.wait_ge(xnT_sb, g0 + gi + 1)
                    for q in range(4):
                        t_.matmul(bank[2][:, (gi * 4 + q) * E:(gi * 4 + q + 1) * E], xngT[:, u, q * P:(q + 1) * P], gate_sb[:],
                                  start=True, stop=True).then_inc(logit_ps, 1)

                groups = TILES // 4
                for gi in range(groups + 1):
                    if gi < groups:
                        transposes(gi, gi % 2)
                    if gi > 0:
                        logits(gi - 1, (gi - 1) % 2)
                pe.wait_ge(hot_done, r + 1)
                hot = ohb[:].rearrange("p t e -> p (t e)")
                t_.matmul(bank[3][:, 0:TILES * E], ones_bf[:], hot, start=True, stop=True)
                t_.matmul(bank[4][:, 0:TILES * E], before[:], hot, start=True, stop=True).then_inc(prefix_ps, 1)
                for c in range(PAIRS):
                    if c % TILES == 0:
                        pe.wait_ge(onehot_done, TOPK * r + c // TILES + 1)
                    ins = t_.matmul(bank[5][:, 0:2 * ETILES], in_tile[:, c, :], which[:, c, :, :].rearrange("p a b -> p (a b)"),
                                    start=(c == 0), stop=(c == PAIRS - 1))
                ins.then_inc(inv_ps, 1)
                pe.wait_ge(route_done, r + 1)
                if r == 0:
                    pe.wait_ge(split_lo, 6)
                k0 = r * ETILES

                def step(k, s, i, loop=False):
                    if on(k, 2, loop):
                        q = (s - 2) % 2
                        pe.reg_load(expert[(s - 2) % 4], etile[0:1, ds(k - 2, 1)])
                        pe.wait_ge(gathered[(s - 2) % 4], dmas(r, i, s - 2))
                        if loop or k >= 4:
                            pe.wait_ge(xl_done, k0 + k - 3)
                        t_.transpose(bank[q][:, 0:P], xr[:, (s - 2) % 4, :], ident[:]).then_inc(xrT_ps, 1)
                    if on(k, 3, loop):
                        q = (s - 3) % 2
                        e = expert_of(s - 3)
                        pe.wait_ge(xl_done, k0 + k - 2)
                        if loop or k >= 5:
                            pe.wait_ge(gelu_done, k0 + k - 4)
                        wh, wl = (w1s[:, ds(e, 1), z, :].rearrange("p a f -> p (a f)") for z in range(2))
                        three(bank[2 + q][:], xh[:, q, :], xl[:, q, :], wh, wl).then_inc(up_ps, 1)
                    if on(k, 4, loop):
                        q = (s - 4) % 2
                        pe.wait_ge(gelu_done, k0 + k - 3)
                        if loop or k >= 6:
                            pe.wait_ge(hl_done, k0 + k - 5)
                        for c in range(FC):
                            ins = t_.transpose(bank[4 + q][:, c * P:(c + 1) * P], hg[:, q, c * P:(c + 1) * P], ident[:])
                        ins.then_inc(hT_ps, 1)
                    if on(k, 5, loop):
                        q = (s - 5) % 2
                        e = expert_of(s - 5)
                        pe.wait_ge(hl_done, k0 + k - 4)
                        if loop or k >= 7:
                            pe.wait_ge(yo_done, k0 + k - 6)
                        for c in range(FC):
                            w = w2s[:, ds(e, 1), c, :].rearrange("p a d -> p (a d)")
                            t_.matmul(bank[6 + q][:, 0:2 * D], hh[:, q, c * P:(c + 1) * P], w, start=(c == 0), stop=False)
                            ins = t_.matmul(bank[6 + q][:, 0:2 * D], hl[:, q, c * P:(c + 1) * P], w, start=False, stop=(c == FC - 1))
                        ins.then_inc(y_ps, 1)

                expert_steps(pe, step)

            def attention_pe(plan, b):
                for task, m, _ in walk(plan, b, "pe"):
                    kind = task[0]
                    if kind == "xT":
                        pe.wait_ge(xa_done, (b + (task[1] + 1)) * QT)
                    if kind in USERS + ("S",):
                        front = front_bank(plan, task)
                        free = front_free(plan, b, task)
                        if free:
                            pe.wait_ge(*free)
                    if kind in ("K", "Q") and ("xT", task[1]) in [x for _, x in plan]:
                        pe.wait_ge(misc_free, place_of(plan, b, ("xT", task[1])))
                    if kind == "xT":
                        for q in range(QT):
                            ins = t_.transpose(front[:, q * P:(q + 1) * P], xa[:, q, :], ident[:])
                    elif kind == "K":
                        ins = three(front[:], wks[:, 0, :], wks[:, 1, :], xTh[:], xTl[:])
                    elif kind == "V":
                        for q in range(QT):
                            c = slice(q * P, (q + 1) * P)
                            ins = three(front[:, q * DH:(q + 1) * DH], xTh[:, c], xTl[:, c], wvs[:, 0, :], wvs[:, 1, :])
                    elif kind == "Q":
                        _, _, g, c = task
                        c = slice((2 * g + c) * P, (2 * g + c + 1) * P)
                        ins = three(front[:], wqs[:, 0, c], wqs[:, 1, c], xTh[:], xTl[:])
                    elif kind == "Y":
                        n = task[1]
                        pe.wait_ge(ot_done, b * NU + (n + 1))
                        for h in range(HG):
                            ins = t_.matmul(OT_BANK[n % 2][:, 0:D], ot[:, n % 2, h * P:(h + 1) * P], wo_sb[:, HG * (n // QT) + h, :],
                                            start=(h == 0), stop=(h == HG - 1))
                        ins.then_inc(proj_ps, 1)
                    if kind in USERS:
                        ins.then_inc(misc_ps, 1)
                    elif kind == "S":
                        _, nb, n, h = task
                        g, t = divmod(n, QT)
                        i = HG * n + h
                        w = max((t + 1) * P, 256)
                        if t == 0 and h == 0:
                            users = [("Q", nb, g, 1)] + ([("K", nb)] if g == 0 else [])
                            tasks = [x for _, x in plan]
                            pe.wait_ge(misc_free, place_of(plan, b, max(users, key=tasks.index)))
                        q = qst[:, g % 2, h, t * P:(t + 1) * P]
                        t_.matmul(front[:, 0:w], q, kst[:, 0, 0:w], start=True, stop=False)
                        t_.matmul(front[:, 0:w], q, kst[:, 1, 0:w], start=False, stop=True).then_inc(s_ps, 1)
                    elif kind == "T":
                        _, n, jj = task
                        i = blk(n, jj)
                        if jj == 0:
                            pe.wait_ge(norm_done, b * NU + (n + 1))
                        if i >= 3:
                            pe.wait_ge(pl_done, b * NB + (i - 2))
                        for h in range(HG):
                            ins = t_.transpose(PT_BANK[i % 3][:, h * P:(h + 1) * P], prob[n % QT][:, h, jj * P:(jj + 1) * P], ident[:])
                        ins.then_inc(pt_ps, 1)
                    elif kind == "AV":
                        _, n, jj = task
                        i = blk(n, jj)
                        pe.wait_ge(pl_done, b * NB + (i + 1))
                        if n == 0 and jj == 0:
                            pe.wait_ge(misc_free, place_of(plan, b, ("V", 0)))
                        if jj == 0 and n >= 2:
                            pe.wait_ge(proj_done, b * NU + (n - 1))
                        t_.matmul(OT_BANK[n % 2][:], vst[:, jj, :], ph[:, i % RING, :], start=(jj == 0), stop=False)
                        t_.matmul(OT_BANK[n % 2][:], vst[:, jj, :], pl[:, i % RING, :], start=False, stop=(jj == n % QT)).then_inc(av_ps, 1)

            ffn_pe(0)
            if stop > 0:
                pe.wait_ge(wa_in, 96)
                attention(pe, attention_pe)
            if stop > 1:
                ffn_pe(1)


_INS = ["L0_attn_x", "L0_attn_Wq", "L0_attn_Wkv", "L0_attn_Wout", "L0_attn_bout", "L0_attn_rel_emb",
        "L0_ffn_gate_w", "L0_ffn_fc_w", "L0_ffn_proj_w"]


def kernel(**inputs):
    import concourse.bacc as bacc
    from concourse.bass_utils import run_bass_kernel_spmd

    nc = bacc.Bacc("TRN2", target_bir_lowering=False, num_devices=1)
    arrays, args = {}, []
    for name in _INS:
        a = np.ascontiguousarray(inputs[name])
        arrays[name] = a
        args.append(nc.dram_tensor(name, a.shape, mybir.dt.from_np(a.dtype), kind="ExternalInput").ap())
    args.append(nc.dram_tensor("out", (BATCH, SEQ, D), F32, kind="ExternalOutput").ap())
    build(nc, *args)
    r = run_bass_kernel_spmd(nc, [arrays], core_ids=[0])
    return r.results[0]["out"]
```
